# Optimizing a Trainium2 kernel written in Bass

```python
import numpy as np
import jax
import jax.numpy as jnp

def _softmax(x, axis=-1):
    return jax.nn.softmax(x, axis=axis)

def _gelu(x):
    return jax.nn.gelu(x, approximate=True)

def _silu(x):
    return jax.nn.silu(x)

def _sigmoid(x):
    return jax.nn.sigmoid(x)

def _layernorm(x, axis=-1, eps=1e-05):
    m = jnp.mean(x, axis=axis, keepdims=True)
    v = jnp.var(x, axis=axis, keepdims=True)
    return (x - m) / jnp.sqrt(v + eps)

def _scatter_add(tgt, idx, src, axis=0):
    return tgt.at[idx].add(src)

def _segment_sum(src, seg, n):
    return jax.ops.segment_sum(src, seg, n)
kernel_name = 'mk_perceiver_d2_seqx_r8_2fafef'

def setup_inputs(seed: int=0):
    np.random.seed(seed)
    _w = jnp.asarray

    def _rec_inputs():
        import jax
        import jax.numpy as jnp
        _rk = jax.random.key(seed)
        x = -0.0002928 + 1 * jax.random.normal(jax.random.fold_in(_rk, 1), (8, 64, 128), jnp.float32)
        _lenS = 64 - jax.random.randint(jax.random.fold_in(_rk, 7), (8,), 0, max(1, 64 // 4) + 1, jnp.int32)
        _lenS2 = 1601 - jax.random.randint(jax.random.fold_in(_rk, 8), (8,), 0, max(1, 1601 // 4) + 1, jnp.int32)
        _ctx_1024P = jax.random.normal(jax.random.fold_in(_rk, 11), (8, 16, 128), jnp.float32)
        _ctx_1024c = jax.random.dirichlet(jax.random.fold_in(_rk, 511), 0.3 * jnp.ones((16,), jnp.float32), (8, 1601))
        _ctx_1024t = jnp.einsum('bsk,bkd->bsd', _ctx_1024c, _ctx_1024P)
        _ctx_1024t = _ctx_1024t * jax.lax.rsqrt(jnp.mean(jnp.square(_ctx_1024t)) + 1e-12) * 0.953939
        ctx_1024 = 0.00222621 + 0.99962 * (_ctx_1024t + 0.3 * jax.random.normal(jax.random.fold_in(_rk, 611), (8, 1601, 128), jnp.float32))
        itok_BxS_0_255 = jax.random.randint(jax.random.fold_in(_rk, 12), (8, 64), 0, 32, jnp.int32)
        _validS = jnp.arange(64)[None, :] < _lenS[:, None]
        _validS2 = jnp.arange(1601)[None, :] < _lenS2[:, None]
        _causal = jnp.tril(jnp.ones((64, 64), dtype=bool))
        mask_BxS2_bk0 = jnp.logical_not(jnp.broadcast_to(_validS2[:, :], (8, 1601)))
        return (x, ctx_1024, itok_BxS_0_255, mask_BxS2_bk0)
    x, ctx_1024, itok_BxS_0_255, mask_BxS2_bk0 = _rec_inputs()

    def _L0_xattn_setup():
        import jax, jax.numpy as jnp
        import numpy as np
        N_LAYERS = 4
        H = 16
        LOOKBACK = 128
        EPS = 1e-06
        ROPE_BASE = 10000.0
        NEG = jnp.float32(-1e+30)

        def rmsnorm(x, w):
            return x * jax.lax.rsqrt(jnp.mean(x * x, axis=-1, keepdims=True) + EPS) * w

        def rope_cache(L, hd):
            inv = 1.0 / ROPE_BASE ** (jnp.arange(0, hd, 2, dtype=jnp.float32) / hd)
            t = jnp.arange(L, dtype=jnp.float32)
            f = t[:, None] * inv[None, :]
            emb = jnp.concatenate([f, f], axis=-1)
            return (jnp.cos(emb), jnp.sin(emb))

        def apply_rope(x, cos, sin):
            d = x.shape[-1]
            x1, x2 = (x[..., :d // 2], x[..., d // 2:])
            rot = jnp.concatenate([-x2, x1], axis=-1)
            return x * cos + rot * sin

        def split_heads(x, n_heads):
            B, L, D = x.shape
            return x.reshape(B, L, n_heads, D // n_heads).transpose(0, 2, 1, 3)

        def merge_heads(x):
            B, h, L, d = x.shape
            return x.transpose(0, 2, 1, 3).reshape(B, L, h * d)

        def sdpa(q, k, v, bias):
            scale = q.shape[-1] ** (-0.5)
            s = jnp.einsum('bhqd,bhkd->bhqk', q, k) * scale + bias
            p = jax.nn.softmax(s, axis=-1)
            return jnp.einsum('bhqk,bhkd->bhqd', p, v)

        def forward(x, memory, seg_ids, Wqkv, bqkv, Wo, bo, Wq_c, Wkv_c, Wo_c, Wg, Wu, Wd, n1, n2, n3, nf):
            B, L, D = x.shape
            S = memory.shape[1]
            hd = D // H
            cos, sin = rope_cache(L, hd)
            i = jnp.arange(L)
            causal_bias = jnp.where(i[None, :] <= i[:, None], 0.0, NEG)[None, None]
            j = jnp.arange(S)
            allowed = (j[None, None, :] <= seg_ids[:, :, None]) & (j[None, None, :] > seg_ids[:, :, None] - LOOKBACK)
            cross_bias = jnp.where(allowed, 0.0, NEG)[:, None]
            for l in range(N_LAYERS):
                h = rmsnorm(x, n1[l])
                qkv = h @ Wqkv[l].T + bqkv[l]
                q, k, v = jnp.split(qkv, 3, axis=-1)
                q = apply_rope(split_heads(q, H), cos, sin)
                k = apply_rope(split_heads(k, H), cos, sin)
                v = split_heads(v, H)
                o = merge_heads(sdpa(q, k, v, causal_bias)) @ Wo[l].T + bo[l]
                x = x + o
                h2 = rmsnorm(x, n2[l])
                qc = split_heads(h2 @ Wq_c[l].T, H)
                kv = memory @ Wkv_c[l].T
                kc, vc = jnp.split(kv, 2, axis=-1)
                kc, vc = (split_heads(kc, H), split_heads(vc, H))
                oc = merge_heads(sdpa(qc, kc, vc, cross_bias)) @ Wo_c[l].T
                x = x + oc
                h3 = rmsnorm(x, n3[l])
                x = x + jax.nn.silu(h3 @ Wg[l].T) * (h3 @ Wu[l].T) @ Wd[l].T
            return rmsnorm(x, nf)
        key = jax.random.key(seed)
        ks = jax.random.split(key, 16)
        B, L, S, D, F = (2, 256, 32, 128, 512)
        w = 0.02
        inp = {'x': jax.random.normal(ks[0], (B, L, D), jnp.float32), 'memory': jax.random.normal(ks[1], (B, S, D), jnp.float32), 'seg_ids': jnp.sort(jax.random.randint(ks[2], (B, L), 0, S), axis=-1), 'Wqkv': jax.random.normal(ks[3], (N_LAYERS, 3 * D, D), jnp.float32) * w, 'bqkv': jnp.zeros((N_LAYERS, 3 * D), jnp.float32), 'Wo': jax.random.normal(ks[4], (N_LAYERS, D, D), jnp.float32) * w, 'bo': jnp.zeros((N_LAYERS, D), jnp.float32), 'Wq_c': jax.random.normal(ks[5], (N_LAYERS, D, D), jnp.float32) * w, 'Wkv_c': jax.random.normal(ks[6], (N_LAYERS, 2 * D, D), jnp.float32) * w, 'Wo_c': jax.random.normal(ks[7], (N_LAYERS, D, D), jnp.float32) * w, 'Wg': jax.random.normal(ks[8], (N_LAYERS, F, D), jnp.float32) * w, 'Wu': jax.random.normal(ks[9], (N_LAYERS, F, D), jnp.float32) * w, 'Wd': jax.random.normal(ks[10], (N_LAYERS, D, F), jnp.float32) * w, 'n1': jnp.ones((N_LAYERS, D), jnp.float32), 'n2': jnp.ones((N_LAYERS, D), jnp.float32), 'n3': jnp.ones((N_LAYERS, D), jnp.float32), 'nf': jnp.ones((D,), jnp.float32)}
        return inp
    _L0_xattn_all = _L0_xattn_setup()
    _L0_xattn_in = {k: v for k, v in _L0_xattn_all.items() if k in ('Wqkv', 'bqkv', 'Wo', 'bo', 'Wq_c', 'Wkv_c', 'Wo_c', 'Wg', 'Wu', 'Wd', 'n1', 'n2', 'n3', 'nf')}
    del _L0_xattn_all

    def _L0_attn_setup():
        import jax, jax.numpy as jnp
        import numpy as np
        BSZ, SEQ, DZ = (4, 256, 128)
        C, R = (16, 64)
        SCALE = 0.03125
        REG_H = 1.0
        key = jax.random.key(seed)
        k1, k2, k3 = jax.random.split(key, 3)
        qz = jax.random.normal(k1, (BSZ, SEQ, DZ), dtype=jnp.float32)
        ternary_factor_u = jax.random.normal(k2, (C * R, DZ), dtype=jnp.float32) * 0.02
        ternary_factor_v = jax.random.normal(k3, (C * R, DZ), dtype=jnp.float32) * 0.02
        return {'qz': qz, 'ternary_factor_u': ternary_factor_u, 'ternary_factor_v': ternary_factor_v}
    _L0_attn_all = _L0_attn_setup()
    _L0_attn_in = {k: v for k, v in _L0_attn_all.items() if k in ('ternary_factor_u', 'ternary_factor_v')}
    del _L0_attn_all

    def _L0_ffn_setup():
        import jax, jax.numpy as jnp
        import numpy as np
        R = 64
        key = jax.random.key(seed)
        k1, k2, k3 = jax.random.split(key, 3)
        B, S, D_IN, D_OUT = (8, 512, 128, 128)
        x = jax.random.normal(k1, (B, S, D_IN), dtype=jnp.float32)
        weight = jax.random.normal(k2, (D_OUT, D_IN), dtype=jnp.float32) * (1.0 / np.sqrt(D_IN))
        disha = jax.random.normal(k3, (R, D_OUT), dtype=jnp.float32) * 0.01
        return {'x': x, 'weight': weight, 'disha': disha}
    _L0_ffn_all = _L0_ffn_setup()
    _L0_ffn_in = {k: v for k, v in _L0_ffn_all.items() if k in ('weight', 'disha')}
    del _L0_ffn_all

    def _L1_xattn_setup():
        import jax, jax.numpy as jnp
        import numpy as np
        DIM = 128
        DIM_LATENT = 128
        DIM_HEAD = 64
        INNER = max(DIM, DIM_LATENT)
        HEADS = INNER // DIM_HEAD
        SCALE = DIM_HEAD ** (-0.5)
        LN_EPS = 1e-05
        RMS_EPS = 1e-08

        def layernorm(x, g, b):
            mu = jnp.mean(x, axis=-1, keepdims=True)
            var = jnp.mean(jnp.square(x - mu), axis=-1, keepdims=True)
            return (x - mu) * jax.lax.rsqrt(var + LN_EPS) * g + b

        def rmsnorm(x, gamma):
            n = jnp.linalg.norm(x, axis=-1, keepdims=True) * x.shape[-1] ** (-0.5)
            return x / jnp.maximum(n, RMS_EPS) * gamma
        key = jax.random.key(seed)
        ks = jax.random.split(key, 8)
        b, n, nl = (8, 256, 64)
        x = jax.random.normal(ks[0], (b, n, DIM), dtype=jnp.float32)
        latents = jax.random.normal(ks[1], (b, nl, DIM_LATENT), dtype=jnp.float32)
        mask = jax.random.randint(ks[2], (b, n), 0, 2).astype(bool)
        init = lambda k, shape, fan_in: jax.random.normal(k, shape, jnp.float32) * fan_in ** (-0.5)
        return {'x': x, 'latents': latents, 'mask': mask, 'ln_x_g': jnp.ones((DIM,), jnp.float32), 'ln_x_b': jnp.zeros((DIM,), jnp.float32), 'ln_l_g': jnp.ones((DIM_LATENT,), jnp.float32), 'ln_l_b': jnp.zeros((DIM_LATENT,), jnp.float32), 'q_gamma': jnp.ones((DIM_HEAD,), jnp.float32), 'k_gamma': jnp.ones((DIM_HEAD,), jnp.float32), 'W_q': init(ks[3], (DIM_LATENT, INNER), DIM_LATENT), 'W_kv': init(ks[4], (DIM, 2 * INNER), DIM), 'W_out': init(ks[5], (INNER, DIM_LATENT), INNER), 'b_out': jnp.zeros((DIM_LATENT,), jnp.float32)}
    _L1_xattn_all = _L1_xattn_setup()
    _L1_xattn_in = {k: v for k, v in _L1_xattn_all.items() if k in ('ln_x_g', 'ln_x_b', 'ln_l_g', 'ln_l_b', 'q_gamma', 'k_gamma', 'W_q', 'W_kv', 'W_out', 'b_out')}
    del _L1_xattn_all

    def _L1_attn_setup():
        import math
        import jax, jax.numpy as jnp
        import numpy as np
        N_HEADS = 16
        THETA = 10000.0

        def _rope_cos_sin(S, head_dim):
            half = head_dim // 2
            inv_freq = 1.0 / THETA ** (jnp.arange(half, dtype=jnp.float32) / half)
            t = jnp.arange(S, dtype=jnp.float32)
            freqs = t[:, None] * inv_freq[None, :]
            return (jnp.cos(freqs), jnp.sin(freqs))

        def _apply_rope(x, cos, sin):
            half = x.shape[-1] // 2
            x1, x2 = (x[..., :half], x[..., half:])
            c = cos[None, None, :, :]
            s = sin[None, None, :, :]
            return jnp.concatenate([x1 * c - x2 * s, x1 * s + x2 * c], axis=-1)
        key = jax.random.key(seed)
        k1, k2, k3 = jax.random.split(key, 3)
        B, S, D = (4, 256, 128)
        x = jax.random.normal(k1, (B, S, D), dtype=jnp.float32)
        w_qkv = jax.random.normal(k2, (3 * D, D), dtype=jnp.float32) * (1.0 / math.sqrt(D))
        w_out = jax.random.normal(k3, (D, D), dtype=jnp.float32) * (1.0 / math.sqrt(D))
        return {'x': x, 'w_qkv': w_qkv, 'w_out': w_out}
    _L1_attn_all = _L1_attn_setup()
    _L1_attn_in = {k: v for k, v in _L1_attn_all.items() if k in ('w_qkv', 'w_out')}
    del _L1_attn_all

    def _L1_ffn_setup():
        import jax, jax.numpy as jnp
        import numpy as np
        HIDDEN = 128
        FFN = 4 * HIDDEN
        NUM_EXPERTS = 8
        TOP_K = 2
        B, S = (4, 256)
        key = jax.random.key(seed)
        ks = jax.random.split(key, 7)
        scale = 0.02
        return {'x': jax.random.normal(ks[0], (B, S, HIDDEN), dtype=jnp.float32), 'gate_w': jax.random.normal(ks[1], (HIDDEN, NUM_EXPERTS), dtype=jnp.float32) * scale, 'gate_b': jnp.zeros((NUM_EXPERTS,), dtype=jnp.float32), 'w1': jax.random.normal(ks[2], (NUM_EXPERTS, HIDDEN, FFN), dtype=jnp.float32) * scale, 'b1': jnp.zeros((NUM_EXPERTS, FFN), dtype=jnp.float32), 'w2': jax.random.normal(ks[3], (NUM_EXPERTS, FFN, HIDDEN), dtype=jnp.float32) * scale, 'b2': jnp.zeros((NUM_EXPERTS, HIDDEN), dtype=jnp.float32)}
    _L1_ffn_all = _L1_ffn_setup()
    _L1_ffn_in = {k: v for k, v in _L1_ffn_all.items() if k in ('gate_w', 'gate_b', 'w1', 'b1', 'w2', 'b2')}
    del _L1_ffn_all
    return {'x': x, 'ctx_1024': ctx_1024, 'itok_BxS_0_255': itok_BxS_0_255, 'mask_BxS2_bk0': mask_BxS2_bk0, 'L0_xattn_Wqkv': _L0_xattn_in['Wqkv'], 'L0_xattn_bqkv': _L0_xattn_in['bqkv'], 'L0_xattn_Wo': _L0_xattn_in['Wo'], 'L0_xattn_bo': _L0_xattn_in['bo'], 'L0_xattn_Wq_c': _L0_xattn_in['Wq_c'], 'L0_xattn_Wkv_c': _L0_xattn_in['Wkv_c'], 'L0_xattn_Wo_c': _L0_xattn_in['Wo_c'], 'L0_xattn_Wg': _L0_xattn_in['Wg'], 'L0_xattn_Wu': _L0_xattn_in['Wu'], 'L0_xattn_Wd': _L0_xattn_in['Wd'], 'L0_xattn_n1': _L0_xattn_in['n1'], 'L0_xattn_n2': _L0_xattn_in['n2'], 'L0_xattn_n3': _L0_xattn_in['n3'], 'L0_xattn_nf': _L0_xattn_in['nf'], 'L0_attn_ternary_factor_u': _L0_attn_in['ternary_factor_u'], 'L0_attn_ternary_factor_v': _L0_attn_in['ternary_factor_v'], 'L0_ffn_weight': _L0_ffn_in['weight'], 'L0_ffn_disha': _L0_ffn_in['disha'], 'L1_xattn_ln_x_g': _L1_xattn_in['ln_x_g'], 'L1_xattn_ln_x_b': _L1_xattn_in['ln_x_b'], 'L1_xattn_ln_l_g': _L1_xattn_in['ln_l_g'], 'L1_xattn_ln_l_b': _L1_xattn_in['ln_l_b'], 'L1_xattn_q_gamma': _L1_xattn_in['q_gamma'], 'L1_xattn_k_gamma': _L1_xattn_in['k_gamma'], 'L1_xattn_W_q': _L1_xattn_in['W_q'], 'L1_xattn_W_kv': _L1_xattn_in['W_kv'], 'L1_xattn_W_out': _L1_xattn_in['W_out'], 'L1_xattn_b_out': _L1_xattn_in['b_out'], 'L1_attn_w_qkv': _L1_attn_in['w_qkv'], 'L1_attn_w_out': _L1_attn_in['w_out'], 'L1_ffn_gate_w': _L1_ffn_in['gate_w'], 'L1_ffn_gate_b': _L1_ffn_in['gate_b'], 'L1_ffn_w1': _L1_ffn_in['w1'], 'L1_ffn_b1': _L1_ffn_in['b1'], 'L1_ffn_w2': _L1_ffn_in['w2'], 'L1_ffn_b2': _L1_ffn_in['b2']}

def reference(x, ctx_1024, itok_BxS_0_255, mask_BxS2_bk0, L0_xattn_Wqkv, L0_xattn_bqkv, L0_xattn_Wo, L0_xattn_bo, L0_xattn_Wq_c, L0_xattn_Wkv_c, L0_xattn_Wo_c, L0_xattn_Wg, L0_xattn_Wu, L0_xattn_Wd, L0_xattn_n1, L0_xattn_n2, L0_xattn_n3, L0_xattn_nf, L0_attn_ternary_factor_u, L0_attn_ternary_factor_v, L0_ffn_weight, L0_ffn_disha, L1_xattn_ln_x_g, L1_xattn_ln_x_b, L1_xattn_ln_l_g, L1_xattn_ln_l_b, L1_xattn_q_gamma, L1_xattn_k_gamma, L1_xattn_W_q, L1_xattn_W_kv, L1_xattn_W_out, L1_xattn_b_out, L1_attn_w_qkv, L1_attn_w_out, L1_ffn_gate_w, L1_ffn_gate_b, L1_ffn_w1, L1_ffn_b1, L1_ffn_w2, L1_ffn_b2):
    import jax
    import jax.numpy as jnp

    def _L0_xattn_ref(x, memory, seg_ids, Wqkv, bqkv, Wo, bo, Wq_c, Wkv_c, Wo_c, Wg, Wu, Wd, n1, n2, n3, nf):
        import jax, jax.numpy as jnp
        import numpy as np
        N_LAYERS = 4
        H = 16
        LOOKBACK = 128
        EPS = 1e-06
        ROPE_BASE = 10000.0
        NEG = jnp.float32(-1e+30)

        def rmsnorm(x, w):
            return x * jax.lax.rsqrt(jnp.mean(x * x, axis=-1, keepdims=True) + EPS) * w

        def rope_cache(L, hd):
            inv = 1.0 / ROPE_BASE ** (jnp.arange(0, hd, 2, dtype=jnp.float32) / hd)
            t = jnp.arange(L, dtype=jnp.float32)
            f = t[:, None] * inv[None, :]
            emb = jnp.concatenate([f, f], axis=-1)
            return (jnp.cos(emb), jnp.sin(emb))

        def apply_rope(x, cos, sin):
            d = x.shape[-1]
            x1, x2 = (x[..., :d // 2], x[..., d // 2:])
            rot = jnp.concatenate([-x2, x1], axis=-1)
            return x * cos + rot * sin

        def split_heads(x, n_heads):
            B, L, D = x.shape
            return x.reshape(B, L, n_heads, D // n_heads).transpose(0, 2, 1, 3)

        def merge_heads(x):
            B, h, L, d = x.shape
            return x.transpose(0, 2, 1, 3).reshape(B, L, h * d)

        def sdpa(q, k, v, bias):
            scale = q.shape[-1] ** (-0.5)
            s = jnp.einsum('bhqd,bhkd->bhqk', q, k) * scale + bias
            p = jax.nn.softmax(s, axis=-1)
            return jnp.einsum('bhqk,bhkd->bhqd', p, v)

        def forward(x, memory, seg_ids, Wqkv, bqkv, Wo, bo, Wq_c, Wkv_c, Wo_c, Wg, Wu, Wd, n1, n2, n3, nf):
            B, L, D = x.shape
            S = memory.shape[1]
            hd = D // H
            cos, sin = rope_cache(L, hd)
            i = jnp.arange(L)
            causal_bias = jnp.where(i[None, :] <= i[:, None], 0.0, NEG)[None, None]
            j = jnp.arange(S)
            allowed = (j[None, None, :] <= seg_ids[:, :, None]) & (j[None, None, :] > seg_ids[:, :, None] - LOOKBACK)
            cross_bias = jnp.where(allowed, 0.0, NEG)[:, None]
            for l in range(N_LAYERS):
                h = rmsnorm(x, n1[l])
                qkv = h @ Wqkv[l].T + bqkv[l]
                q, k, v = jnp.split(qkv, 3, axis=-1)
                q = apply_rope(split_heads(q, H), cos, sin)
                k = apply_rope(split_heads(k, H), cos, sin)
                v = split_heads(v, H)
                o = merge_heads(sdpa(q, k, v, causal_bias)) @ Wo[l].T + bo[l]
                x = x + o
                h2 = rmsnorm(x, n2[l])
                qc = split_heads(h2 @ Wq_c[l].T, H)
                kv = memory @ Wkv_c[l].T
                kc, vc = jnp.split(kv, 2, axis=-1)
                kc, vc = (split_heads(kc, H), split_heads(vc, H))
                oc = merge_heads(sdpa(qc, kc, vc, cross_bias)) @ Wo_c[l].T
                x = x + oc
                h3 = rmsnorm(x, n3[l])
                x = x + jax.nn.silu(h3 @ Wg[l].T) * (h3 @ Wu[l].T) @ Wd[l].T
            return rmsnorm(x, nf)
        return forward(x, memory, seg_ids, Wqkv, bqkv, Wo, bo, Wq_c, Wkv_c, Wo_c, Wg, Wu, Wd, n1, n2, n3, nf)

    def _L0_attn_ref(qz, ternary_factor_u, ternary_factor_v):
        import jax, jax.numpy as jnp
        import numpy as np
        BSZ, SEQ, DZ = (4, 256, 128)
        C, R = (16, 64)
        SCALE = 0.03125
        REG_H = 1.0
        bsz, seq_len, _ = qz.shape
        qz_u = qz @ ternary_factor_u.T * SCALE
        qz_v = qz @ ternary_factor_v.T * SCALE
        qz_u = qz_u.reshape(bsz, seq_len, C, R).transpose(0, 2, 1, 3)
        qz_v = qz_v.reshape(bsz, seq_len, C, R).transpose(0, 2, 1, 3)
        message_F = jnp.einsum('bcsr,bctr->bcst', qz_u, qz_v)
        qh = jax.nn.sigmoid(message_F / REG_H)
        qh_v1 = jnp.einsum('bcst,bctr->bcsr', qh, qz_v)
        qh_v2 = jnp.einsum('bcst,bcsr->bctr', qh, qz_u)
        qh_v1 = qh_v1.transpose(0, 2, 1, 3).reshape(bsz, seq_len, C * R)
        qh_v2 = qh_v2.transpose(0, 2, 1, 3).reshape(bsz, seq_len, C * R)
        message_G = (qh_v1 @ ternary_factor_u + qh_v2 @ ternary_factor_v) * SCALE
        return message_G

    def _L0_ffn_ref(x, weight, disha):
        import jax, jax.numpy as jnp
        import numpy as np
        R = 64
        result = jnp.einsum('bsd,od->bso', x, weight)
        r = disha.shape[0]
        pooled = x.reshape(*x.shape[:-1], x.shape[-1] // r, r).sum(axis=-2)
        return result + pooled @ disha

    def _L1_xattn_ref(x, latents, mask, ln_x_g, ln_x_b, ln_l_g, ln_l_b, q_gamma, k_gamma, W_q, W_kv, W_out, b_out):
        import jax, jax.numpy as jnp
        import numpy as np
        DIM = 128
        DIM_LATENT = 128
        DIM_HEAD = 64
        INNER = max(DIM, DIM_LATENT)
        HEADS = INNER // DIM_HEAD
        SCALE = DIM_HEAD ** (-0.5)
        LN_EPS = 1e-05
        RMS_EPS = 1e-08

        def layernorm(x, g, b):
            mu = jnp.mean(x, axis=-1, keepdims=True)
            var = jnp.mean(jnp.square(x - mu), axis=-1, keepdims=True)
            return (x - mu) * jax.lax.rsqrt(var + LN_EPS) * g + b

        def rmsnorm(x, gamma):
            n = jnp.linalg.norm(x, axis=-1, keepdims=True) * x.shape[-1] ** (-0.5)
            return x / jnp.maximum(n, RMS_EPS) * gamma
        b, n, _ = x.shape
        nl = latents.shape[1]
        xn = layernorm(x, ln_x_g, ln_x_b)
        ln = layernorm(latents, ln_l_g, ln_l_b)
        q = ln @ W_q
        kv = jnp.concatenate([xn @ W_kv, ln @ W_kv], axis=1)
        k, v = (kv[..., :INNER], kv[..., INNER:])
        to_heads = lambda t: t.reshape(t.shape[0], t.shape[1], HEADS, DIM_HEAD).transpose(0, 2, 1, 3)
        q, k, v = (to_heads(q), to_heads(k), to_heads(v))
        qn = rmsnorm(q, q_gamma) * SCALE
        kn = rmsnorm(k, k_gamma)
        sim = jnp.einsum('bhid,bhjd->bhij', qn, kn)
        full_mask = jnp.pad(mask, ((0, 0), (0, nl)), constant_values=True)
        neg = -jnp.finfo(sim.dtype).max
        sim = jnp.where(full_mask[:, None, None, :], sim, neg)
        attn = jax.nn.softmax(sim.astype(jnp.float32), axis=-1).astype(sim.dtype)
        out = jnp.einsum('bhij,bhjd->bhid', attn, v)
        out = out.transpose(0, 2, 1, 3).reshape(b, nl, INNER)
        return out @ W_out + b_out

    def _L1_attn_ref(x, w_qkv, w_out):
        import math
        import jax, jax.numpy as jnp
        import numpy as np
        N_HEADS = 16
        THETA = 10000.0

        def _rope_cos_sin(S, head_dim):
            half = head_dim // 2
            inv_freq = 1.0 / THETA ** (jnp.arange(half, dtype=jnp.float32) / half)
            t = jnp.arange(S, dtype=jnp.float32)
            freqs = t[:, None] * inv_freq[None, :]
            return (jnp.cos(freqs), jnp.sin(freqs))

        def _apply_rope(x, cos, sin):
            half = x.shape[-1] // 2
            x1, x2 = (x[..., :half], x[..., half:])
            c = cos[None, None, :, :]
            s = sin[None, None, :, :]
            return jnp.concatenate([x1 * c - x2 * s, x1 * s + x2 * c], axis=-1)
        B, S, D = x.shape
        H = N_HEADS
        hd = D // H
        qkv = x @ w_qkv.T
        q, k, v = jnp.split(qkv, 3, axis=-1)

        def reshape(t):
            return t.reshape(B, S, H, hd).transpose(0, 2, 1, 3)
        q, k, v = (reshape(q), reshape(k), reshape(v))
        cos, sin = _rope_cos_sin(S, hd)
        q = _apply_rope(q.astype(jnp.float32), cos, sin).astype(x.dtype)
        k = _apply_rope(k.astype(jnp.float32), cos, sin).astype(x.dtype)
        scale = math.sqrt(hd)
        scores = jnp.einsum('bhsd,bhtd->bhst', q, k) / scale
        causal = jnp.tril(jnp.ones((S, S), dtype=bool))
        scores = jnp.where(causal[None, None], scores, -jnp.inf)
        attn = jax.nn.softmax(scores.astype(jnp.float32), axis=-1).astype(x.dtype)
        out = jnp.einsum('bhst,bhtd->bhsd', attn, v)
        out = out.transpose(0, 2, 1, 3).reshape(B, S, D)
        return out @ w_out.T

    def _L1_ffn_ref(x, gate_w, gate_b, w1, b1, w2, b2):
        import jax, jax.numpy as jnp
        import numpy as np
        HIDDEN = 128
        FFN = 4 * HIDDEN
        NUM_EXPERTS = 8
        TOP_K = 2
        B, S = (4, 256)
        b, s, h = x.shape
        xt = x.reshape(b * s, h)
        probs = jax.nn.softmax(xt @ gate_w + gate_b, axis=-1)
        _, idx = jax.lax.top_k(probs, TOP_K)
        one_hot = jax.nn.one_hot(idx, NUM_EXPERTS, dtype=xt.dtype)
        mask = (one_hot.sum(axis=1) > 0).astype(xt.dtype)
        h1 = jax.nn.relu(jnp.einsum('th,ehf->etf', xt, w1) + b1[:, None, :])
        out_e = jnp.einsum('etf,efh->eth', h1, w2) + b2[:, None, :]
        out = jnp.einsum('eth,te->th', out_e, mask)
        return out.reshape(b, s, h)
    x = x + _L0_xattn_ref(_layernorm(x, axis=-1), ctx_1024, itok_BxS_0_255, L0_xattn_Wqkv, L0_xattn_bqkv, L0_xattn_Wo, L0_xattn_bo, L0_xattn_Wq_c, L0_xattn_Wkv_c, L0_xattn_Wo_c, L0_xattn_Wg, L0_xattn_Wu, L0_xattn_Wd, L0_xattn_n1, L0_xattn_n2, L0_xattn_n3, L0_xattn_nf)
    x = x + _L0_attn_ref(_layernorm(x, axis=-1), L0_attn_ternary_factor_u, L0_attn_ternary_factor_v)
    x = x + _L0_ffn_ref(_layernorm(x, axis=-1), L0_ffn_weight, L0_ffn_disha)
    x = x + _L1_xattn_ref(ctx_1024, _layernorm(x, axis=-1), mask_BxS2_bk0, L1_xattn_ln_x_g, L1_xattn_ln_x_b, L1_xattn_ln_l_g, L1_xattn_ln_l_b, L1_xattn_q_gamma, L1_xattn_k_gamma, L1_xattn_W_q, L1_xattn_W_kv, L1_xattn_W_out, L1_xattn_b_out)
    x = x + _L1_attn_ref(_layernorm(x, axis=-1), L1_attn_w_qkv, L1_attn_w_out)
    x = x + _L1_ffn_ref(_layernorm(x, axis=-1), L1_ffn_gate_w, L1_ffn_gate_b, L1_ffn_w1, L1_ffn_b1, L1_ffn_w2, L1_ffn_b2)
    return x

_drawn_inputs = setup_inputs


def setup_inputs(seed=0):
    import zlib

    import numpy as np

    out = dict(_drawn_inputs(seed))
    spreads = {'L0_xattn_bqkv': (0.0, 0.337),
     'L0_xattn_bo': (0.0, 0.1),
     'L0_xattn_n1': (1.0, 0.6),
     'L0_xattn_n2': (1.0, 0.6),
     'L0_xattn_n3': (1.0, 0.6),
     'L0_xattn_nf': (1.0, 0.2),
     'L1_xattn_ln_x_g': (1.0, 0.2),
     'L1_xattn_ln_x_b': (0.0, 0.1),
     'L1_xattn_ln_l_g': (1.0, 0.6),
     'L1_xattn_ln_l_b': (0.0, 0.424),
     'L1_xattn_q_gamma': (1.0, 0.6),
     'L1_xattn_k_gamma': (1.0, 0.6),
     'L1_xattn_b_out': (0.0, 0.1),
     'L1_ffn_gate_b': (0.0, 0.1),
     'L1_ffn_b1': (0.0, 0.442),
     'L1_ffn_b2': (0.0, 0.1)}
    factors = {'L0_xattn_Wqkv': 3.127,
     'L0_xattn_Wq_c': 29.654,
     'L0_xattn_Wg': 4.085,
     'L0_xattn_Wu': 3.964,
     'L0_xattn_Wd': 3.996,
     'L0_attn_ternary_factor_u': 8.0,
     'L0_attn_ternary_factor_v': 8.0}
    for name, (base, spread) in spreads.items():
        noise = np.random.default_rng([zlib.crc32(name.encode()), seed]).standard_normal(out[name].shape)
        drawn = base * np.exp(spread * noise) if base else spread * noise
        out[name] = jnp.asarray(drawn.astype(out[name].dtype))
    for name, factor in factors.items():
        out[name] = (out[name] * factor).astype(out[name].dtype)
    return out
```

```python
from contextlib import ExitStack

import numpy as np
import concourse.bass as bass
from concourse import mybir

F32 = mybir.dt.float32
BF16 = mybir.dt.bfloat16
I32 = mybir.dt.int32
U32 = mybir.dt.uint32
U8 = mybir.dt.uint8
ALU = mybir.AluOpType
ACT = mybir.ActivationFunctionType
AX = mybir.AxisListType.X

P = 128
B, L, D = 8, 64, 128
T = B * L // P
LAYERS = 4
H, HD = 16, 8
F = 512
FC = F // P
S2 = 1601
KF = 32
CT = (S2 + P - 1) // P
CR = S2 - (CT - 1) * P
LOOKBACK = 128
RMS_EPS = 1e-6
NEG = -1e30
RMS_FLOOR = 1e-16
C, R = 16, 64
UV_SCALE = 0.03125
XH, XD = 2, 64
E = 8
ds = bass.ds

A_Q, A_QR, A_K, A_KR, A_V, A_O = (i * P for i in range(6))
A_N1 = 6 * P
A_BQ, A_BQR, A_BK, A_BKR, A_BV = (A_N1 + 1 + i for i in range(5))
A_COLS = A_N1 + 6
B_Q, B_K, B_V, B_O = (i * P for i in range(4))
B_N2 = 4 * P
B_COLS = B_N2 + 1
C_G, C_U, C_D = 0, F, 2 * F
C_N3 = 3 * F
C_COLS = C_N3 + 1

X_Q, X_K, X_V, X_KT, X_O = (i * P for i in range(5))
X_GX, X_BX, X_GL, X_BL, X_GQ, X_GK = (5 * P + i for i in range(6))
X_COLS = 5 * P + 6
W_1, W_2, W_B1 = 0, F, 2 * F
W_COLS = 2 * F + FC
CG = [range(c, min(c + 4, CT)) for c in range(0, CT, 4)]

(NORM1, TRH1, PROJ, SCORE, PTR, PV, TRO1, OUT1, TRH2, QC, CSCORE, CPTR, CPV, TRO2, OUT2, TRH3, UP,
 DOWN) = range(18)
SELF = range(NORM1, OUT1 + 1)
KINDS = {
    "norm": (NORM1, OUT1, OUT2),
    "tr": (TRH1, TRO1, TRH2, TRO2, TRH3),
    "yp": (OUT1, OUT2, DOWN),
    "pt": (PTR, CPTR),
    "pv": (PV, CPV),
    "sm": (SCORE, CSCORE),
    "q": (PROJ, QC),
    "qc": (QC,),
    "small": (TRH1, PV, TRO1, OUT1, TRH2, QC, CPV, TRO2, OUT2, TRH3, DOWN),
}


class Order:

    def __init__(self, parts, last=False):
        self.steps = []
        for part in parts:
            part = list(part)
            for slot in range(len(part) + T - 1):
                self.steps += [(part[slot - t], t) for t in range(T) if 0 <= slot - t < len(part)]
        self.last = last

    def at(self, kind, stage, t):
        steps = [x for x in self.steps if x[0] in KINDS[kind]]
        return steps.index((stage, t))

    def count(self, kind, stage, t, l):
        return l * (len(KINDS[kind]) * T) + self.at(kind, stage, t) + 1


FAST = Order([range(18)])
GENERAL = Order([range(QC + 1), range(CSCORE, TRO2), range(TRO2, 18)])
LAST = Order([SELF])


CREDIT = {"tr_taken": 5 * T, "o_ready": 2 * T, "y_ready": 3 * T, "qc_taken": T, "pt_taken_act": 1,
          "pt_taken_dve": 1, "hidden_ready": T}
TAKEN = {"tr": "tr_taken", "pv": "o_ready", "yp": "y_ready", "qc": "qc_taken"}


def one(l, t):
    return l * T + t + 1


def program(nc, x_in, seg_in, segq_in, ctx_in, ctxT_in, memT_in, wa_in, bo_in, wb_in, wc_in, nf_in,
            trig_in, cf_in, cb_in, iota_in, uvT_in, uv_in, ffw_in, xw_in, bout_in, eye2_in, mask_in, sel_in, gate_in, b2_in, we_in, out, stop=99):
    with ExitStack() as ctx:
        def sb(name, shape, dt=F32):
            return ctx.enter_context(nc.sbuf_tensor(name, shape, dt))

        def sem(name):
            return ctx.enter_context(nc.semaphore(name))

        sc = [ctx.enter_context(nc.psum_tensor(f"sc{i}", [P, 1024], F32)) for i in range(2)]
        pt = ctx.enter_context(nc.psum_tensor("pt", [P, 1024], F32))
        small = [ctx.enter_context(nc.psum_tensor(f"small{i}", [P, 512], F32)) for i in range(2)]

        x = sb("x", [P, T, D])
        h = sb("h", [P, T, D])
        sq = sb("sq", [P, T, D + 1])
        ss = sb("ss", [P, T])
        lg = sb("lg", [P, T])
        rstd = sb("rstd", [P, T])
        h2 = sb("h2", [P, T, 2, 2, L])
        hT = sb("hT", [P, T, P])
        st = sb("st", [P, T, 6])
        mv = sb("mv", [P, T, 2])
        par = sb("par", [P, 3])
        wa = sb("wa", [P, A_COLS])
        bo = sb("bo", [P, D])
        trig = sb("trig", [P, 4, P])
        cf = sb("cf", [P, 155])
        ident = cf[:, 0:128]
        hm4 = cf[:, 128:132]
        vm2 = cf[:, 132:134]
        vm4 = cf[:, 134:138]
        hm16 = cf[:, 138:154]
        jcol = cf[0:KF, 154:155]
        cb = sb("cb", [64, P + 1024], BF16)
        causal = cb[:, 0:P]
        it64 = cb[:, P:P + 512]
        it32 = cb[0:KF, P + 512:P + 1024]
        rope = sb("rope", [P, T, 4, P])
        qT = sb("qT", [P, T, P])
        q4 = sb("q4", [P, T, 4, P])
        kT = sb("kT", [P, T, P])
        kblk = sb("kblk", [P, T, 2, 4, L])
        vblk = sb("vblk", [P, T, 2, 8, 2, 9])
        mx = sb("mx", [P, T, H])
        sd = sb("sd", [P, T, 1024])
        pr = sb("pr", [P, T, 1024])
        pts = sb("pts", [P, T, 1024])
        rv = sb("rv", [P, T, H])
        o = sb("o", [P, T, D])
        oT = sb("oT", [P, T, P])

        l0 = ctx.enter_context(ExitStack())

        def lsb(name, shape, dt=F32):
            return l0.enter_context(nc.sbuf_tensor(name, shape, dt))

        y = lsb("y", [P, T, D + 1])
        yb = lsb("yb", [P, T, D])
        wb = lsb("wb", [P, B_COLS])
        wc = lsb("wc", [P, C_COLS])
        nf = lsb("nf", [P, D])
        memT = lsb("memT", [P, B, KF])
        mem4 = lsb("mem4", [P, B, 4, KF])
        kcT = lsb("kcT", [P, B, KF])
        kcblk = lsb("kcblk", [P, B, 4, KF])
        vcblk = lsb("vcblk", [P, B, 4, 4, 9])
        segr = lsb("segr", [KF, B * L], I32)
        segf = lsb("segf", [KF, B * L])
        cmask = lsb("cmask", [KF, B * L], BF16)
        seg1 = lsb("seg1", [1, 4])
        flag = lsb("flag", [1, 1], I32)

        names = ("loaded wa_loaded wb_loaded wc_loaded ones_set h_doubled prep_done seg_cast cmask_ready iota_loaded uv_loaded ffn_loaded seg_range seg_far flag_ready "
                 "ln_stats ln_moments ln_log ln_rstd ln_done "
                 "squares_summed rstd_ready h_ready tr_ready tr_taken proj_ready v_ready rope_terms "
                 "v_taken yb_ready q_ready q_summed k_summed k_ready scores_ready max_ready shifted probs_ready pt_ready "
                 "pt_taken_act pt_taken_dve pv_ready rv_ready o_ready yp_ready y_ready qc_ready qc_taken "
                 "mem_k_ready mem_k_taken kc_ready mem_v_ready vc_ready gate_ready up_ready tanh_ready "
                 "gated hidden_ready final_scaled final_h x_ready stored wa_free wb_free wc_free "
                 ).split()
        s = {n: sem(n) for n in names}

        early = ctx.enter_context(ExitStack())
        gsem = {n: early.enter_context(nc.semaphore("any_" + n)) for n in (
            "ctx_loaded k_ps k_ready v_ps v_taken seg_low low_mask in_window bias_ready q_ready s_ps biased max_ready "
            "shifted exp_ready pt_ps pt_taken o_ps recip_ready o_taken iota_ready").split()}
        g = ctx.enter_context(ExitStack())

        def gsb(name, shape, dt=F32):
            return g.enter_context(nc.sbuf_tensor(name, shape, dt))

        cT = gsb("cT", [P, S2])
        kcf = gsb("kcf", [P, S2])
        vcf = gsb("vcf", [P, CT, P])
        iota = gsb("iota", [L, S2])
        win = gsb("win", [L, S2])
        bias = gsb("bias", [L, S2])
        sg = gsb("sg", [L, S2])
        pg = gsb("pg", [L, S2])
        ptg = gsb("ptg", [P, CT, L])
        qg = gsb("qg", [P, L])
        segq = gsb("segq", [L, B], I32)
        seghi = gsb("seghi", [L, B])
        seglo = gsb("seglo", [L, B])
        mg = gsb("mg", [L, 1])
        sumg = gsb("sumg", [L, 1])
        rg = gsb("rg", [L, 1])
        g.close()

        uvT = lsb("uvT", [P, 2, C * R])
        uv = lsb("uv", [P, 2, 8, D])
        ffw = lsb("ffw", [P, 2, D])
        wide = "p w (j q) -> p w j q"
        ut = sd[:, 0:2, :].rearrange(wide, q=P)
        un = sd[:, 2:4, :]
        th = pr[:, 0:2, :]
        qh = pr[:, 2:4, :].rearrange("p w (a j q) -> p w a j q", a=2, q=L)
        v12 = pts[:, 0:2, :].rearrange("p w (j b q) -> p w j b q", b=2, q=L)
        l0.close()

        x1 = ctx.enter_context(ExitStack())

        def xsb(name, shape, dt=F32):
            return x1.enter_context(nc.sbuf_tensor(name, shape, dt))

        xw = xsb("xw", [P, X_COLS])
        bout = xsb("bout", [P, D])
        eye2 = xsb("eye2", [P, L])
        mraw = xsb("mraw", [B, CT * P], U8)
        notm = xsb("notm", [B, CT * P], BF16)
        sel = xsb("sel", [B, B, P], BF16)
        gqk = xsb("gqk", [P, 1])
        bxb = xsb("bxb", [P, P])
        bwv = xsb("bwv", [P, P])
        sqx = xsb("sqx", [P, 1024])
        ssq = xsb("ssq", [P, 16])
        rqk = xsb("rqk", [P, 16])
        qnat = xsb("qnat", [P, T, P])
        qp = xsb("qp", [P, B, XH, L])
        vl = xsb("vl", [P, T, P])
        vlc = [xsb(f"vlc{i}", [P, P]) for i in range(2)]
        slt = xsb("slt", [P, T, P])
        slat = xsb("slat", [P, T, P])
        cx = [xsb(f"cx{i}", [P, CT, D]) for i in range(2)]
        xh = [xsb(f"xh{i}", [P, CT, D]) for i in range(2)]
        stx = xsb("stx", [P, CT, 6])
        mvx = [xsb(f"mvx{i}", [P, CT, 2]) for i in range(2)]
        lgx = xsb("lgx", [P, CT])
        rsx = [xsb(f"rsx{i}", [P, CT]) for i in range(2)]
        xnT = [xsb(f"xnT{i}", [P, 512]) for i in range(2)]
        ksq = [xsb(f"ksq{i}", [P, 512]) for i in range(2)]
        kss = [xsb(f"kss{i}", [P, 8]) for i in range(2)]
        kfl = [xsb(f"kfl{i}", [P, 8]) for i in range(2)]
        rk = [xsb(f"rk{i}", [P, 8]) for i in range(2)]
        sT = xsb("sT", [P, CT, P])
        mxx = xsb("mxx", [P, 3])
        mx1 = xsb("mx1", [P, 1])
        nmx = [xsb(f"nmx{i}", [P, 1]) for i in range(2)]
        pn = [xsb(f"pn{i}", [P, (CT + 1) * P]) for i in range(2)]
        rsum = [xsb(f"rsum{i}", [P, 3]) for i in range(2)]
        rc = xsb("rc", [P, 2])
        rs4 = xsb("rs4", [P, 2, 2])
        ptx = xsb("ptx", [P, CT + 1, P])
        utx = xsb("utx", [P, P])
        rec = xsb("rec", [P, 2])
        o1 = xsb("o1", [P, P])
        o2 = xsb("o2", [P, P])
        ox = xsb("ox", [P, P])
        oTx = xsb("oTx", [P, P])
        x1.close()

        m1 = ctx.enter_context(ExitStack())

        def msb(name, shape, dt=F32):
            return m1.enter_context(nc.sbuf_tensor(name, shape, dt))

        gate = msb("gate", [P, 3 * E])
        b2 = msb("b2", [E, D])
        we = [msb(f"we{i}", [P, W_COLS]) for i in range(2)]
        lgt = msb("lgt", [P, T, E])
        gmx = msb("gmx", [P, T])
        gsh = msb("gsh", [P, T, E])
        gex = msb("gex", [P, T, E])
        gsum = msb("gsum", [P, T])
        grec = msb("grec", [P, T])
        prob = [msb(f"prob{i}", [P, T, E]) for i in range(2)]
        best = msb("best", [P, T])
        rank = msb("rank", [P, T, E])
        first = msb("first", [P, T])
        picked = [msb(f"picked{i}", [P, T, E]) for i in range(2)]
        chosen = msb("chosen", [P, T, E])
        choT = msb("choT", [E, T, P])
        hid = [msb(f"hid{i}", [P, FC, T * P]) for i in range(2)]
        m1.close()

        def load_a(sp, l):
            sp.dma_start(wa[:], wa_in[ds(l, 1)].rearrange("a p n -> p (a n)")).then_inc(s["wa_loaded"], 16)
            sp.dma_start(bo[:], bo_in[ds(l, 1), :].to_broadcast([P, D])).then_inc(s["wa_loaded"], 16)

        def load_b(sp, l):
            sp.dma_start(wb[:], wb_in[ds(l, 1)].rearrange("a p n -> p (a n)")).then_inc(s["wb_loaded"], 16)

        def load_c(sp, l):
            sp.dma_start(wc[:], wc_in[ds(l, 1)].rearrange("a p n -> p (a n)")).then_inc(s["wc_loaded"], 16)

        am = {n: early.enter_context(nc.semaphore("l0_" + n)) for n in (
            "zT_ps zT_ready uT_ps uT_half uT_taken un_ps un_half un_taken M_ps M_taken MT_taken qh_ready v12_ps "
            "v2_taken v12_taken G_ps G_taken F_ps F_taken").split()}

        xw_loaded = sem("xw_loaded")
        gate_loaded = sem("gate_loaded")
        expert_loaded = [sem(f"expert_loaded{i}") for i in range(2)]
        ctx_loaded = [sem(f"ctx_tiles_loaded{i}") for i in range(2)]

        def layernorm_dve(dve, k, src, dst, done=None):
            for t in range(T):
                nc.vector.bn_stats(st[:, t, :], src[:, t, :]).then_inc(s["ln_stats"], 1)
            dve.wait_ge(s["ln_stats"], T * (k + 1))
            for t in range(T):
                nc.vector.bn_aggr(mv[:, t, :], st[:, t, :]).then_inc(s["ln_moments"], 1)
            dve.wait_ge(s["ln_rstd"], k + 1)
            for t in range(T):
                nc.vector.tensor_scalar(dst[:, t, 0:D], src[:, t, :], mv[:, t, 0:1], rstd[:, t:t + 1],
                                        ALU.subtract, ALU.mult).then_inc(s["ln_done"] if done is None else done, 1)

        def layernorm_pool(pool, k):
            pool.wait_ge(s["prep_done"], 1)
            pool.wait_ge(s["ln_moments"], T * (k + 1))
            nc.gpsimd.tensor_tensor(lg[:], mv[:, :, 1], par[:, 0:1].to_broadcast([P, T]), ALU.add).then_inc(s["ln_log"], 1)
            pool.wait_ge(s["ln_log"], k + 1)
            nc.gpsimd.tensor_tensor(rstd[:], lg[:], par[:, 1:2].to_broadcast([P, T]), ALU.pow).then_inc(s["ln_rstd"], 1)

        block = nc.Block()
        block.__enter__()

        @block.sync
        def _(sp):
            sp.dma_start(x[:], x_in.rearrange("(t p) d -> p t d", p=P)).then_inc(s["loaded"], 16)
            sp.dma_start(segr[:], seg_in.to_broadcast([KF, B * L])).then_inc(s["loaded"], 16)
            sp.dma_start(cf[:], cf_in).then_inc(s["loaded"], 16)
            sp.dma_start(cb[:], cb_in).then_inc(s["loaded"], 16)
            sp.dma_start(trig[:], trig_in).then_inc(s["loaded"], 16)
            sp.dma_start(memT[:], memT_in).then_inc(s["loaded"], 16)
            sp.dma_start(nf[:], nf_in.to_broadcast([P, D])).then_inc(s["loaded"], 16)
            sp.dma_start(segq[:], segq_in).then_inc(s["loaded"], 16)
            load_a(sp, 0)
            load_b(sp, 0)
            load_c(sp, 0)

        @block.gpsimd
        def _(pool):
            nc.gpsimd.memset(vblk[:], 0.0).then_inc(s["ones_set"], 1)
            nc.gpsimd.memset(vcblk[:], 0.0).then_inc(s["ones_set"], 1)
            pool.wait_ge(s["loaded"], 16 * 8)
            nc.gpsimd.tensor_copy(mem4[:], memT[:].unsqueeze(2).to_broadcast([P, B, 4, KF])).then_inc(s["ones_set"], 1)
            layernorm_pool(pool, 0)

        @block.scalar
        def _(act):
            nc.scalar.preload_act_table_set("exp_and_others")

        @block.vector
        def _(dve):
            dve.wait_ge(s["ones_set"], 2)
            for a in range(2):
                nc.vector.memset(vblk[64 * a:64 * a + 64, :, :, :, a, 8:9], 1.0)
            for a in range(4):
                nc.vector.memset(vcblk[32 * a:32 * a + 32, :, :, a, 8:9], 1.0)
            nc.vector.memset(par[:, 0:1], 1e-5)
            nc.vector.memset(par[:, 1:2], -0.5)
            nc.vector.memset(par[:, 2:3], 1.0)
            nc.vector.memset(y[:, :, D:D + 1], (RMS_EPS * D) ** 0.5).then_inc(s["prep_done"], 1)
            for name, n in CREDIT.items():
                dve.sem_inc(s[name], n)
            for name in sorted(set(gsem) - {"ctx_loaded"}):
                dve.sem_inc(gsem[name], 1)
            for name in sorted(am):
                dve.sem_inc(am[name], 2)
            dve.wait_ge(s["loaded"], 16 * 8)
            nc.vector.tensor_copy(segf[:], segr[:]).then_inc(s["seg_cast"], 1)
            nc.vector.tensor_copy(seghi[:], segq[:]).then_inc(s["seg_cast"], 1)
            dve.wait_ge(s["seg_cast"], 2)
            nc.vector.tensor_scalar(seglo[:], seghi[:], float(LOOKBACK), None, ALU.subtract).then_inc(gsem["seg_low"], 1)
            nc.vector.tensor_scalar(cmask[:], segf[:], jcol, NEG, ALU.is_lt, ALU.mult).then_inc(s["cmask_ready"], 1)
            nc.vector.tensor_reduce(seg1[:, 0:1], segf[0:1, :], AX, ALU.max).then_inc(s["seg_range"], 1)
            nc.vector.tensor_reduce(seg1[:, 1:2], segf[0:1, :], AX, ALU.min).then_inc(s["seg_range"], 1)
            dve.wait_ge(s["seg_range"], 2)
            nc.vector.tensor_scalar(seg1[:, 2:3], seg1[:, 0:1], float(KF), None, ALU.is_lt).then_inc(s["seg_far"], 1)
            nc.vector.tensor_scalar(seg1[:, 3:4], seg1[:, 1:2], 0.0, None, ALU.is_ge).then_inc(s["seg_far"], 1)
            dve.wait_ge(s["seg_far"], 2)
            nc.vector.tensor_tensor(flag[:], seg1[:, 2:3], seg1[:, 3:4], ALU.mult).then_inc(s["flag_ready"], 1)
            layernorm_dve(dve, 0, x, y)

        block.__exit__(None, None, None)

        pe_stage, act_stage, dve_stage, pool_stage = {}, {}, {}, {}

        def bank_of(od, stage, t):
            return small[od.at("small", stage, t) % 2]

        def small_wait(pe, od, stage, t, l):
            steps = [x for x in od.steps if x[0] in KINDS["small"]]
            n = od.at("small", stage, t) - 2
            if n < 0 and od is LAST:
                return
            before, tile = steps[n]
            kind = next(k for k in TAKEN if before in KINDS[k])
            pe.wait_ge(s[TAKEN[kind]], taken(TAKEN[kind], od, kind, before, tile, l if n >= 0 else l - 1))

        def taken(name, od, kind, stage, t, l):
            return od.count(kind, stage, t, l) + CREDIT[name]

        def pe_transpose(pe, od, stage, l, t, src):
            small_wait(pe, od, stage, t, l)
            nc.tensor.transpose(bank_of(od, stage, t)[:, 0:P], src[:, t, :], ident).then_inc(s["tr_ready"], 1)

        def pe_trh(pe, od, stage, l, t):
            norm = {TRH1: NORM1, TRH2: OUT1, TRH3: OUT2}[stage]
            pe.wait_ge(s["h_ready"], od.count("norm", norm, t, l))
            pe_transpose(pe, od, stage, l, t, h)

        def pe_tro(pe, od, stage, l, t):
            pe.wait_ge(s["o_ready"], taken("o_ready", od, "pv", PV if stage == TRO1 else CPV, t, l))
            pe_transpose(pe, od, stage, l, t, o)

        def pe_proj(pe, od, stage, l, t):
            pe.wait_ge(s["tr_taken"], taken("tr_taken", od, "tr", TRH1, t, l))
            if t >= 2:
                pe.wait_ge(s["shifted"], od.count("sm", SCORE, t - 2, l))
            else:
                pe.wait_ge(s["hidden_ready"], l * T + T)
            if t == 0:
                pe.wait_ge(s["wa_loaded"], 32 * (l + 1))
            if t == 1 and od is FAST:
                pe.wait_ge(s["mem_k_taken"], l + 1)
            for i, w in enumerate((A_Q, A_QR, A_K, A_KR)):
                last = nc.tensor.matmul(sc[t % 2][:, P * i:P * i + P], wa[:, w:w + P], hT[:, t, :], start=True, stop=True)
            last.then_inc(s["proj_ready"], 1)
            pe.wait_ge(s["h_doubled"], one(l, t))
            for b in range(2):
                last = nc.tensor.matmul(sc[t % 2][:, 512 + P * b:512 + P * b + P], h2[:, t, b, :, :].rearrange("p a q -> p (a q)"), wa[:, A_V:A_V + P], start=True, stop=True)
            last.then_inc(s["v_ready"], 1)

        def pe_score(pe, od, stage, l, t):
            pe.wait_ge(s["rope_terms"], one(l, t))
            pe.wait_ge(s["v_taken"], one(l, t))
            for i in range(2):
                nc.tensor.matmul(sc[t % 2][:, 512 * i:512 * i + 512], causal, it64, start=True, stop=True)
            pe.wait_ge(s["q_ready"], od.count("q", PROJ, t, l))
            pe.wait_ge(s["k_ready"], one(l, t))
            for b in range(2):
                for g in range(4):
                    last = nc.tensor.matmul(sc[t % 2][L * b:L * b + L, 256 * g:256 * g + 256],
                                            q4[:, t, g, L * b:L * b + L], kblk[:, t, b, :, :],
                                            start=False, stop=True, skip_group_check=True)
            last.then_inc(s["scores_ready"], 1)

        def pt_wait(pe, od, stage, l, t):
            pe.wait_ge(s["pt_taken_act"], taken("pt_taken_act", od, "pt", stage, t, l) - 1)
            pe.wait_ge(s["pt_taken_dve"], taken("pt_taken_dve", od, "pt", stage, t, l) - 1)

        def pe_ptr(pe, od, stage, l, t):
            pe.wait_ge(s["probs_ready"], od.count("sm", SCORE if stage == PTR else CSCORE, t, l))
            pt_wait(pe, od, stage, l, t)
            if t == 0 and stage == PTR and od is FAST:
                pe.wait_ge(s["vc_ready"], l + 1)
            n = 4 if stage == PTR else 2
            for i in range(2):
                for j in range(n):
                    c = P * (n * i + j)
                    last = nc.tensor.transpose(pt[:, 512 * i + P * j:512 * i + P * j + P], pr[:, t, c:c + P], ident)
                last.then_inc(s["pt_ready"], 1)

        def pv_wait(pe, od, stage, l, t):
            pe.wait_ge(s["pt_taken_act"], taken("pt_taken_act", od, "pt", PTR if stage == PV else CPTR, t, l))
            pe.wait_ge(s["pt_taken_dve"], taken("pt_taken_dve", od, "pt", PTR if stage == PV else CPTR, t, l))
            small_wait(pe, od, stage, t, l)

        def pe_pv(pe, od, stage, l, t):
            pv_wait(pe, od, stage, l, t)
            ops = bank_of(od, stage, t)
            for b in range(2):
                for j in range(8):
                    last = nc.tensor.matmul(ops[L * b:L * b + L, 18 * j:18 * j + 18], pts[:, t, P * j + L * b:P * j + L * b + L],
                                            vblk[:, t, b, j, :, :], start=True, stop=True)
            last.then_inc(s["pv_ready"], 1)

        def pe_out(pe, od, stage, l, t):
            tro, w = (TRO1, wa[:, A_O:A_O + P]) if stage == OUT1 else (TRO2, wb[:, B_O:B_O + P])
            pe.wait_ge(s["tr_taken"], taken("tr_taken", od, "tr", tro, t, l))
            small_wait(pe, od, stage, t, l)
            nc.tensor.matmul(bank_of(od, stage, t)[:, 0:P], oT[:, t, :], w, start=True, stop=True).then_inc(s["yp_ready"], 1)

        def pe_qc(pe, od, stage, l, t):
            pe.wait_ge(s["tr_taken"], taken("tr_taken", od, "tr", TRH2, t, l))
            small_wait(pe, od, stage, t, l)
            if t == 0:
                pe.wait_ge(s["wb_loaded"], 16 * (l + 1))
            nc.tensor.matmul(bank_of(od, stage, t)[:, 0:P], wb[:, B_Q:B_Q + P], hT[:, t, :], start=True, stop=True).then_inc(s["qc_ready"], 1)

        def pe_cscore(pe, od, stage, l, t):
            pe.wait_ge(s["shifted"], od.count("sm", SCORE, t + 2, l) if t < 2 else od.count("sm", CSCORE, t - 2, l))
            nc.tensor.matmul(sc[t % 2][:, 0:512], cmask[:, P * t:P * t + P], it32, start=True, stop=True)
            pe.wait_ge(s["q_ready"], od.count("q", QC, t, l))
            pe.wait_ge(s["kc_ready"], l + 1)
            for b in range(2):
                for g in range(4):
                    last = nc.tensor.matmul(sc[t % 2][L * b:L * b + L, P * g:P * g + P], q4[:, t, g, L * b:L * b + L],
                                            kcblk[:, 2 * t + b, :, :], start=False, stop=True, skip_group_check=True)
            last.then_inc(s["scores_ready"], 1)

        def pe_cpv(pe, od, stage, l, t):
            pv_wait(pe, od, stage, l, t)
            pe.wait_ge(s["vc_ready"], l + 1)
            ops = bank_of(od, stage, t)
            for b in range(2):
                for g in range(4):
                    last = nc.tensor.matmul(ops[L * b:L * b + L, 36 * g:36 * g + 36], pts[:, t, P * g + L * b:P * g + L * b + L],
                                            vcblk[:, 2 * t + b, g, :, :], start=True, stop=True)
            last.then_inc(s["pv_ready"], 1)

        def pe_up(pe, od, stage, l, t):
            pe.wait_ge(s["tr_taken"], taken("tr_taken", od, "tr", TRH3, t, l))
            if t == 0:
                pe.wait_ge(s["wc_loaded"], 16 * (l + 1))
            if t >= 2:
                pe.wait_ge(s["hidden_ready"], one(l, t - 2) + T)
            else:
                pe.wait_ge(s["shifted"], 2 * T * (l + 1))
            for i, (w, done) in enumerate(((C_G, "gate_ready"), (C_U, "up_ready"))):
                for c in range(FC):
                    last = nc.tensor.matmul(sc[t % 2][:, 512 * i + P * c:512 * i + P * c + P],
                                            wc[:, w + P * c:w + P * c + P], hT[:, t, :], start=True, stop=True)
                last.then_inc(s[done], 1)

        def pe_down(pe, od, stage, l, t):
            pe.wait_ge(s["hidden_ready"], one(l, t) + T)
            small_wait(pe, od, stage, t, l)
            for c in range(FC):
                last = nc.tensor.matmul(bank_of(od, stage, t)[:, 0:P], sd[:, t, 512 + P * c:512 + P * c + P],
                                        wc[:, C_D + P * c:C_D + P * c + P], start=(c == 0), stop=(c == FC - 1))
            last.then_inc(s["yp_ready"], 1)

        pe_stage.update({TRH1: pe_trh, PROJ: pe_proj, SCORE: pe_score, PTR: pe_ptr, PV: pe_pv, TRO1: pe_tro, OUT1: pe_out,
                         TRH2: pe_trh, QC: pe_qc, CSCORE: pe_cscore, CPTR: pe_ptr, CPV: pe_cpv, TRO2: pe_tro, OUT2: pe_out,
                         TRH3: pe_trh, UP: pe_up, DOWN: pe_down})

        def act_norm(act, od, stage, l, t):
            n = od.count("norm", stage, t, l)
            if stage == NORM1:
                act.wait_ge(s["y_ready"], taken("y_ready", od, "yp", DOWN, t, l) - 3 * T)
            else:
                act.wait_ge(s["y_ready"], taken("y_ready", od, "yp", stage, t, l))
            nc.scalar.activation(sq[:, t, :], y[:, t, :], ACT.Square, scale=D ** -0.5,
                                 accum_out=ss[:, t:t + 1]).then_inc(s["squares_summed"], 1)

        def act_trh(act, od, stage, l, t):
            w = {TRH1: wa[:, A_N1:A_N1 + 1], TRH2: wb[:, B_N2:B_N2 + 1], TRH3: wc[:, C_N3:C_N3 + 1]}[stage]
            if t == 0:
                act.wait_ge(s[{TRH1: "wa_loaded", TRH2: "wb_loaded", TRH3: "wc_loaded"}[stage]],
                            (32 if stage == TRH1 else 16) * (l + 1))
            act.wait_ge(s["tr_ready"], od.count("tr", stage, t, l))
            nc.scalar.activation(hT[:, t, :], bank_of(od, stage, t)[:, 0:P], ACT.Copy, scale=w).then_inc(s["tr_taken"], 1)

        def act_tro(act, od, stage, l, t):
            act.wait_ge(s["tr_ready"], od.count("tr", stage, t, l))
            src = bank_of(od, stage, t)[:, 0:P]
            if stage == TRO1:
                nc.scalar.activation(oT[:, t, :], src, ACT.Identity, bias=wa[:, A_BV:A_BV + 1]).then_inc(s["tr_taken"], 1)
            else:
                nc.scalar.copy(oT[:, t, :], src).then_inc(s["tr_taken"], 1)

        def act_exp(act, od, stage, l, t):
            n = 1024 if stage == SCORE else 512
            act.wait_ge(s["shifted"], od.count("sm", stage, t, l))
            nc.scalar.activation(pr[:, t, 0:n], sd[:, t, 0:n], ACT.Exp).then_inc(s["probs_ready"], 1)

        def act_ptr(act, od, stage, l, t):
            n = 512 if stage == PTR else 256
            act.wait_ge(s["pt_ready"], 2 * od.count("pt", stage, t, l) - 1)
            nc.scalar.copy(pts[:, t, 0:n], pt[:, 0:n]).then_inc(s["pt_taken_act"], 1)

        def act_qc(act, od, stage, l, t):
            act.wait_ge(s["qc_ready"], one(l, t))
            nc.scalar.mul(qT[:, t, :], bank_of(od, stage, t)[:, 0:P], HD ** -0.5).then_inc(s["qc_taken"], 1)

        def act_up(act, od, stage, l, t):
            act.wait_ge(s["gate_ready"], one(l, t))
            nc.scalar.activation(pr[:, t, 0:F], sc[t % 2][:, 0:F], ACT.Tanh, scale=0.5).then_inc(s["tanh_ready"], 1)

        act_stage.update({NORM1: act_norm, OUT1: act_norm, OUT2: act_norm, TRH1: act_trh, SCORE: act_exp, PTR: act_ptr, TRO1: act_tro, TRH2: act_trh,
                          QC: act_qc, CSCORE: act_exp, CPTR: act_ptr, TRO2: act_tro, TRH3: act_trh, UP: act_up})

        def dve_proj(dve, od, stage, l, t):
            dve.wait_ge(s["proj_ready"], one(l, t))
            for i, b in enumerate((A_BQ, A_BQR, A_BK, A_BKR)):
                last = nc.vector.scalar_tensor_tensor(rope[:, t, i, :], sc[t % 2][:, P * i:P * i + P], wa[:, b:b + 1],
                                                      trig[:, i, :], ALU.add, ALU.mult)
            last.then_inc(s["rope_terms"], 1)
            dve.wait_ge(s["v_ready"], one(l, t))
            nc.vector.tensor_tensor(
                vblk[:, t, :, :, :, 0:8].rearrange("p b j a d -> p (b j) a d"),
                sc[t % 2][:, 512:768].rearrange("p (j a d) -> p j a d", a=2, d=8),
                vm2.unsqueeze(1).unsqueeze(3).to_broadcast([P, 16, 2, 8]), ALU.mult).then_inc(s["v_taken"], 1)

        def dve_score(dve, od, stage, l, t):
            k = L if stage == SCORE else KF
            n = od.count("sm", stage, t, l)
            scores = sc[t % 2][:, 0:H * k].rearrange("p (h k) -> p h k", k=k)
            dve.wait_ge(s["scores_ready"], n)
            nc.vector.tensor_reduce(mx[:, t, :], scores, AX, ALU.max).then_inc(s["max_ready"], 1)
            dve.wait_ge(s["max_ready"], n)
            nc.vector.tensor_tensor(sd[:, t, 0:H * k].rearrange("p (h k) -> p h k", k=k), scores,
                                    mx[:, t, :].unsqueeze(2).to_broadcast([P, H, k]), ALU.subtract).then_inc(s["shifted"], 1)

        def dve_ptr(dve, od, stage, l, t):
            n = 512 if stage == PTR else 256
            dve.wait_ge(s["pt_ready"], 2 * od.count("pt", stage, t, l))
            nc.vector.tensor_copy(pts[:, t, n:2 * n], pt[:, 512:512 + n]).then_inc(s["pt_taken_dve"], 1)

        def dve_pv(dve, od, stage, l, t):
            n = od.count("pv", stage, t, l)
            ops = bank_of(od, stage, t)[:, 0:144].rearrange("p (h e) -> p h e", e=9)
            dve.wait_ge(s["pv_ready"], n)
            nc.vector.reciprocal(rv[:, t, :], ops[:, :, 8]).then_inc(s["rv_ready"], 1)
            dve.wait_ge(s["rv_ready"], n)
            nc.vector.tensor_tensor(o[:, t, :].rearrange("p (h d) -> p h d", d=HD), ops[:, :, 0:8],
                                    rv[:, t, :].unsqueeze(2).to_broadcast([P, H, HD]), ALU.mult).then_inc(s["o_ready"], 1)

        def dve_y(dve, od, stage, l, t):
            base, dst = y, y
            if od is LAST:
                base, dst = x, x
            elif stage == OUT1:
                dve.wait_ge(s["yb_ready"], one(l, t))
                base = yb
            elif stage == OUT2:
                dve.wait_ge(s["y_ready"], od.count("yp", OUT1, t, l) + CREDIT["y_ready"])
            else:
                dve.wait_ge(s["y_ready"], od.count("yp", OUT2, t, l) + CREDIT["y_ready"])
            dve.wait_ge(s["yp_ready"], od.count("yp", stage, t, l))
            nc.vector.tensor_tensor(dst[:, t, 0:D], bank_of(od, stage, t)[:, 0:P], base[:, t, 0:D], ALU.add).then_inc(s["y_ready"], 1)

        def dve_up(dve, od, stage, l, t):
            n = one(l, t)
            dve.wait_ge(s["tanh_ready"], n)
            nc.vector.scalar_tensor_tensor(sd[:, t, 0:F], pr[:, t, 0:F], 1.0, sc[t % 2][:, 0:F], ALU.add,
                                           ALU.mult).then_inc(s["gated"], 1)
            dve.wait_ge(s["up_ready"], n)
            dve.wait_ge(s["gated"], n)
            nc.vector.scalar_tensor_tensor(sd[:, t, F:2 * F], sd[:, t, 0:F], 0.5, sc[t % 2][:, F:2 * F], ALU.mult,
                                           ALU.mult).then_inc(s["hidden_ready"], 1)

        dve_stage.update({PROJ: dve_proj, SCORE: dve_score, PTR: dve_ptr, PV: dve_pv, OUT1: dve_y, CSCORE: dve_score,
                          CPTR: dve_ptr, CPV: dve_pv, OUT2: dve_y, UP: dve_up, DOWN: dve_y})

        def pool_norm(pool, od, stage, l, t):
            n = od.count("norm", stage, t, l)
            pool.wait_ge(s["squares_summed"], n)
            nc.gpsimd.tensor_tensor(rstd[:, t:t + 1], ss[:, t:t + 1], par[:, 1:2], ALU.pow).then_inc(s["rstd_ready"], 1)
            pool.wait_ge(s["rstd_ready"], n)
            nc.gpsimd.tensor_tensor(h[:, t, :], y[:, t, 0:D], rstd[:, t:t + 1].to_broadcast([P, D]), ALU.mult).then_inc(s["h_ready"], 1)
            if stage == NORM1:
                if t == 0:
                    pool.wait_ge(s["wa_loaded"], 32 * (l + 1))
                nc.gpsimd.tensor_tensor(yb[:, t, :], y[:, t, 0:D], bo[:], ALU.add).then_inc(s["yb_ready"], 1)

        def pool_proj(pool, od, stage, l, t):
            n = one(l, t)
            pool.wait_ge(s["rope_terms"], n)
            nc.gpsimd.tensor_tensor(qT[:, t, :], rope[:, t, 0, :], rope[:, t, 1, :], ALU.add).then_inc(s["q_summed"], 1)
            nc.gpsimd.tensor_tensor(kT[:, t, :], rope[:, t, 2, :], rope[:, t, 3, :], ALU.add).then_inc(s["k_summed"], 1)
            pool.wait_ge(s["q_summed"], n)
            pool_groups(pool, t)
            pool.wait_ge(s["k_summed"], n)
            for b in range(2):
                last = nc.gpsimd.tensor_tensor(kblk[:, t, b, :, :],
                                               kT[:, t, L * b:L * b + L].unsqueeze(1).to_broadcast([P, 4, L]),
                                               hm4.unsqueeze(2).to_broadcast([P, 4, L]), ALU.mult)
            last.then_inc(s["k_ready"], 1)

        def pool_groups(pool, t):
            nc.gpsimd.tensor_tensor(q4[:, t, :, :], qT[:, t, :].unsqueeze(1).to_broadcast([P, 4, P]),
                                    vm4.unsqueeze(2).to_broadcast([P, 4, P]), ALU.mult).then_inc(s["q_ready"], 1)

        def pool_qc(pool, od, stage, l, t):
            pool.wait_ge(s["qc_taken"], one(l, t) + CREDIT["qc_taken"])
            pool_groups(pool, t)

        def pool_double(pool, od, stage, l, t):
            pool.wait_ge(s["tr_taken"], taken("tr_taken", od, "tr", TRH1, t, l))
            twice = hT[:, t, :].rearrange("p (b q) -> p b q", q=L).unsqueeze(2).to_broadcast([P, 2, 2, L])
            nc.gpsimd.tensor_tensor(h2[:, t, :, :, :], twice, par[:, 2:3].unsqueeze(2).unsqueeze(3).to_broadcast([P, 2, 2, L]),
                                    ALU.mult).then_inc(s["h_doubled"], 1)

        pool_stage.update({TRH1: pool_double, QC: pool_qc, NORM1: pool_norm, PROJ: pool_proj, OUT1: pool_norm, OUT2: pool_norm})

        ends = {LAST: (act_norm, pool_norm)}

        def layer(table, eng, od, l, stages=range(18)):
            for stage, t in od.steps:
                if stage in stages and stage in table and table[stage] not in ends.get(od, ()):
                    table[stage](eng, od, stage, l, t)

        def pe_memory(pe, l):
            pe.wait_ge(s["wb_loaded"], 16 * (l + 1))
            pe.wait_ge(s["hidden_ready"], l * T + CREDIT["hidden_ready"])
            nc.tensor.matmul(sc[1][:, 0:256], wb[:, B_K:B_K + P], memT[:].rearrange("p b k -> p (b k)"),
                             start=True, stop=True).then_inc(s["mem_k_ready"], 1)
            pe.wait_ge(s["pt_taken_act"], l * (2 * T) + CREDIT["pt_taken_act"])
            pe.wait_ge(s["pt_taken_dve"], l * (2 * T) + CREDIT["pt_taken_dve"])
            for b in range(B):
                last = nc.tensor.matmul(pt[:, P * b:P * b + P], mem4[:, b, :, :].rearrange("p i k -> p (i k)"), wb[:, B_V:B_V + P], start=True, stop=True)
            last.then_inc(s["mem_v_ready"], 1)

        def act_memory(act, l):
            act.wait_ge(s["mem_k_ready"], l + 1)
            nc.scalar.copy(kcT[:].rearrange("p b k -> p (b k)"), sc[1][:, 0:256]).then_inc(s["mem_k_taken"], 1)

        def pool_memory(pool, l):
            pool.wait_ge(s["mem_k_taken"], l + 1)
            for b in range(B):
                last = nc.gpsimd.tensor_tensor(kcblk[:, b, :, :], kcT[:, b, :].unsqueeze(1).to_broadcast([P, 4, KF]),
                                               hm4.unsqueeze(2).to_broadcast([P, 4, KF]), ALU.mult)
            last.then_inc(s["kc_ready"], 1)

        def dve_memory(dve, l):
            dve.wait_ge(s["mem_v_ready"], l + 1)
            nc.vector.tensor_tensor(
                vcblk[:, :, :, :, 0:8].rearrange("p b g i d -> p (b g) i d"),
                pt[:].rearrange("p (g i d) -> p g i d", i=4, d=8),
                vm4.unsqueeze(1).unsqueeze(3).to_broadcast([P, 32, 4, 8]), ALU.mult).then_inc(s["vc_ready"], 1)


        def each_batch(eng, l, body):
            with eng.Fori(0, T) as t:
                for b in range(2):
                    body((l * T + t) * 2 + b, t, b)

        def sp_any(sp, l):
            def batch(i, t, b):
                sp.wait_ge(gsem["v_taken"], 2 * i + 1)
                sp.dma_start(cT[:], ctxT_in[ds(2 * t + b, 1)].rearrange("a p s -> p (a s)")).then_inc(gsem["ctx_loaded"], 16)
            each_batch(sp, l, batch)

        def pe_any(pe, l):
            def batch(i, t, b):
                pe.wait_ge(s["qc_taken"], T * (l + 1) + CREDIT["qc_taken"])
                pe.wait_ge(s["shifted"], l * (2 * T) + T)
                pe.wait_ge(s["o_ready"], l * (2 * T) + T + CREDIT["o_ready"])
                pe.wait_ge(s["tr_taken"], l * (5 * T) + 3 * T + CREDIT["tr_taken"])
                pe.wait_ge(s["y_ready"], l * (3 * T) + T + CREDIT["y_ready"])
                pe.wait_ge(s["pt_taken_act"], l * (2 * T) + T + CREDIT["pt_taken_act"])
                pe.wait_ge(s["pt_taken_dve"], l * (2 * T) + T + CREDIT["pt_taken_dve"])
                pe.wait_ge(gsem["ctx_loaded"], 16 * (i + 1))
                pe.wait_ge(gsem["biased"], 2 * H * i + 1)
                for c in range(4):
                    n = min(512, S2 - 512 * c)
                    last = nc.tensor.matmul(sc[c // 2][:, 512 * (c % 2):512 * (c % 2) + n], wb[:, B_K:B_K + P],
                                            cT[:, 512 * c:512 * c + n], start=True, stop=True)
                last.then_inc(gsem["k_ps"], 1)
                pe.wait_ge(gsem["pt_taken"], H * i + 1)
                for r, tiles in enumerate((range(8), range(8, CT))):
                    pe.wait_ge(gsem["v_taken"], 2 * i + r + 1)
                    for c in tiles:
                        n = P if c < CT - 1 else CR
                        last = nc.tensor.matmul(pt[0:n, P * (c % 8):P * (c % 8) + P], cT[:, P * c:P * c + n],
                                                wb[:, B_V:B_V + P], start=True, stop=True)
                    last.then_inc(gsem["v_ps"], 1)
                with pe.Fori(0, H) as hh:
                    j = i * H + hh
                    pe.wait_ge(gsem["k_ready"], i + 2)
                    pe.wait_ge(gsem["v_taken"], 2 * i + 3)
                    pe.wait_ge(gsem["q_ready"], j + 2)
                    pe.wait_ge(gsem["biased"], 2 * j + 1)
                    for c in range(4):
                        n = min(512, S2 - 512 * c)
                        last = nc.tensor.matmul(sc[c // 2][0:L, 512 * (c % 2):512 * (c % 2) + n], qg[:],
                                                kcf[:, 512 * c:512 * c + n], start=True, stop=True)
                    last.then_inc(gsem["s_ps"], 1)
                    pe.wait_ge(gsem["exp_ready"], j + 2)
                    pe.wait_ge(gsem["pt_taken"], j + 1)
                    for c in range(CT):
                        n = P if c < CT - 1 else CR
                        last = nc.tensor.matmul(pt[0:n, L * c:L * c + L], pg[:, P * c:P * c + n], ident[0:L, 0:L],
                                                start=True, stop=True)
                    last.then_inc(gsem["pt_ps"], 1)
                    pe.wait_ge(gsem["pt_taken"], j + 2)
                    pe.wait_ge(gsem["o_taken"], j + 1)
                    for c in range(CT):
                        n = P if c < CT - 1 else CR
                        last = nc.tensor.matmul(small[0][0:L, 0:P], ptg[0:n, c, :], vcf[0:n, c, :],
                                                start=(c == 0), stop=(c == CT - 1))
                    last.then_inc(gsem["o_ps"], 1)
            each_batch(pe, l, batch)
            for name, n in (("scores_ready", T), ("pt_ready", 2 * T), ("pv_ready", T)):
                pe.sem_inc(s[name], n)

        def act_any(act, l):
            def batch(i, t, b):
                act.wait_ge(gsem["k_ps"], i + 2)
                nc.scalar.copy(kcf[:, 0:1024], sc[0][:])
                nc.scalar.copy(kcf[:, 1024:S2], sc[1][:, 0:S2 - 1024]).then_inc(gsem["k_ready"], 1)
                with act.Fori(0, H) as hh:
                    j = i * H + hh
                    act.wait_ge(gsem["shifted"], j + 2)
                    act.wait_ge(gsem["o_taken"], j + 1)
                    nc.scalar.activation(pg[:], sg[:], ACT.Exp, accum_out=sumg[:]).then_inc(gsem["exp_ready"], 1)
                    act.wait_ge(gsem["pt_ps"], j + 2)
                    nc.scalar.copy(ptg[0:CR, CT - 1, :], pt[0:CR, L * (CT - 1):L * CT])
                    nc.scalar.copy(ptg[:, 0:CT - 1, :].rearrange("p c q -> p (c q)"), pt[:, 0:L * (CT - 1)]).then_inc(gsem["pt_taken"], 1)
            each_batch(act, l, batch)
            for name, n in (("probs_ready", T), ("pt_taken_act", T)):
                act.sem_inc(s[name], n)

        def dve_any(dve, l):
            def batch(i, t, b):
                dve.wait_ge(gsem["seg_low"], 2)
                dve.wait_ge(s["iota_loaded"], 16)
                dve.wait_ge(gsem["biased"], 2 * H * i + 1)
                nc.vector.tensor_scalar(win[:], iota[:], seghi[:, ds(2 * t + b, 1)], None, ALU.is_le).then_inc(gsem["low_mask"], 1)
                dve.wait_ge(gsem["low_mask"], i + 2)
                nc.vector.scalar_tensor_tensor(bias[:], iota[:], seglo[:, ds(2 * t + b, 1)], win[:], ALU.is_gt,
                                               ALU.mult).then_inc(gsem["in_window"], 1)
                dve.wait_ge(gsem["in_window"], i + 2)
                nc.vector.tensor_scalar(bias[:], bias[:], 1.0, -NEG, ALU.subtract, ALU.mult).then_inc(gsem["bias_ready"], 1)
                for r, tiles in enumerate((range(8), range(8, CT))):
                    dve.wait_ge(gsem["v_ps"], 2 * i + r + 2)
                    if r == 0:
                        nc.vector.tensor_copy(vcf[:, 0:8, :], pt[:].rearrange("p (c d) -> p c d", d=P)).then_inc(gsem["v_taken"], 1)
                    else:
                        nc.vector.tensor_copy(vcf[:, 8:CT - 1, :], pt[:, 0:P * (CT - 9)].rearrange("p (c d) -> p c d", d=P))
                        nc.vector.tensor_copy(vcf[0:CR, CT - 1, :], pt[0:CR, P * (CT - 9):P * (CT - 8)]).then_inc(gsem["v_taken"], 1)
                with dve.Fori(0, H) as hh:
                    j = i * H + hh
                    dve.wait_ge(gsem["bias_ready"], i + 2)
                    dve.wait_ge(gsem["s_ps"], j + 1)
                    nc.vector.tensor_scalar(qg[:], qT[:, ds(t, 1), L * b:L * b + L].rearrange("p a q -> p (a q)"),
                                            hm16[:, ds(hh, 1)], None, ALU.mult).then_inc(gsem["q_ready"], 1)
                    dve.wait_ge(gsem["s_ps"], j + 2)
                    for c, (a, e) in enumerate(((0, 1024), (1024, S2))):
                        nc.vector.tensor_tensor(sg[:, a:e], sc[c][0:L, 0:e - a], bias[:, a:e], ALU.add).then_inc(gsem["biased"], 1)
                    dve.wait_ge(gsem["biased"], 2 * j + 2 + 1)
                    nc.vector.tensor_reduce(mg[:], sg[:], AX, ALU.max).then_inc(gsem["max_ready"], 1)
                    dve.wait_ge(gsem["max_ready"], j + 2)
                    nc.vector.tensor_scalar(sg[:], sg[:], mg[:, 0:1], None, ALU.subtract).then_inc(gsem["shifted"], 1)
                    dve.wait_ge(gsem["exp_ready"], j + 2)
                    nc.vector.reciprocal(rg[:], sumg[:]).then_inc(gsem["recip_ready"], 1)
                    dve.wait_ge(gsem["recip_ready"], j + 2)
                    dve.wait_ge(gsem["o_ps"], j + 2)
                    nc.vector.tensor_scalar(o[L * b:L * b + L, ds(t, 1), ds(hh * HD, HD)].rearrange("p a d -> p (a d)"),
                                            small[0][0:L, ds(hh * HD, HD)], rg[:, 0:1], None, ALU.mult).then_inc(gsem["o_taken"], 1)
            each_batch(dve, l, batch)
            for name in ("max_ready", "shifted", "pt_taken_dve", "rv_ready"):
                dve.sem_inc(s[name], T)
            dve.wait_ge(gsem["o_taken"], H * B * (l + 1) + 1)
            dve.sem_inc(s["o_ready"], T)

        def run(table, eng, l, general, memory=None, whole=None):
            if general:
                layer(table, eng, GENERAL, l, range(QC + 1))
                if whole is not None:
                    whole(eng, l)
                layer(table, eng, GENERAL, l, range(TRO2, 18))
            else:
                if memory is not None:
                    memory(eng, l)
                layer(table, eng, FAST, l)

        def both(eng, table, memory, whole):
            fast = eng.value_load(flag[0:1, 0:1], min_val=0, max_val=1)
            with eng.If(fast == 1):
                with eng.Fori(0, LAYERS) as l:
                    run(table, eng, l, False, memory, whole)
            with eng.Else():
                with eng.Fori(0, LAYERS) as l:
                    run(table, eng, l, True, memory, whole)

        def sp_layers(sp, l, general):
            if general:
                sp_any(sp, l)
            sp.wait_ge(s["y_ready"], FAST.count("yp", OUT1, T - 1, l) + CREDIT["y_ready"])
            load_a(sp, l + 1)
            if isinstance(l, int) and l == LAYERS - 1:
                return
            sp.wait_ge(s["y_ready"], FAST.count("yp", OUT2, T - 1, l) + CREDIT["y_ready"])
            load_b(sp, l + 1)
            sp.wait_ge(s["y_ready"], FAST.count("yp", DOWN, T - 1, l) + CREDIT["y_ready"])
            load_c(sp, l + 1)

        def load_uv(sp):
            sp.dma_start(uvT[:], uvT_in).then_inc(s["uv_loaded"], 16)
            sp.dma_start(uv[:], uv_in).then_inc(s["uv_loaded"], 16)
            sp.dma_start(ffw[:], ffw_in).then_inc(s["uv_loaded"], 16)

        with nc.Block() as block:
            @block.sync
            def _(sp):
                fast = sp.value_load(flag[0:1, 0:1], min_val=0, max_val=1)
                with sp.If(fast == 1):
                    load_uv(sp)
                    with sp.Fori(0, LAYERS - 1) as l:
                        sp_layers(sp, l, False)
                    sp_layers(sp, LAYERS - 1, False)
                with sp.Else():
                    sp.dma_start(iota[:], iota_in.to_broadcast([L, S2])).then_inc(s["iota_loaded"], 16)
                    with sp.Fori(0, LAYERS - 1) as l:
                        sp_layers(sp, l, True)
                    sp_layers(sp, LAYERS - 1, True)
                    sp.wait_ge(s["y_ready"], FAST.count("yp", DOWN, T - 1, LAYERS - 1) + CREDIT["y_ready"])
                    load_uv(sp)

            @block.tensor
            def _(pe):
                both(pe, pe_stage, pe_memory, pe_any)

            @block.scalar
            def _(act):
                both(act, act_stage, act_memory, act_any)
                for t in range(T):
                    act.wait_ge(s["y_ready"], FAST.count("yp", DOWN, t, LAYERS - 1) + CREDIT["y_ready"])
                    nc.scalar.activation(sq[:, t, :], y[:, t, :], ACT.Square, scale=D ** -0.5,
                                         accum_out=ss[:, t:t + 1]).then_inc(s["squares_summed"], 1)

            @block.vector
            def _(dve):
                both(dve, dve_stage, dve_memory, dve_any)
                dve.wait_ge(s["rstd_ready"], 3 * T * LAYERS + 1)
                for t in range(T):
                    nc.vector.scalar_tensor_tensor(h[:, t, :], y[:, t, 0:D], rstd[:, t:t + 1], nf[:], ALU.mult,
                                                   ALU.mult).then_inc(s["final_scaled"], 1)
                dve.wait_ge(s["final_scaled"], T)
                nc.vector.tensor_tensor(x[:], x[:], h[:], ALU.add).then_inc(s["x_ready"], 1)

            @block.gpsimd
            def _(pool):
                both(pool, pool_stage, pool_memory, None)
                pool.wait_ge(s["squares_summed"], 3 * T * LAYERS + T)
                nc.gpsimd.tensor_tensor(rstd[:], ss[:], par[:, 1:2].to_broadcast([P, T]), ALU.pow).then_inc(s["rstd_ready"], 1)

        def store_now():
            with nc.Block() as block:
                @block.sync
                def _(sp):
                    sp.wait_ge(s["wa_loaded"], 32 * 5)
                    sp.dma_start(out.rearrange("(t p) d -> p t d", p=P), x[:]).then_inc(s["stored"], 16)
                    sp.wait_ge(s["stored"], 16)

        if stop == 1:
            return store_now()

        def nth(k, back=0):
            return k + 3 - back

        def am_pe(pe):
            for t in range(T):
                pe.wait_ge(s["ln_done"], T + t + 1)
                if t >= 2:
                    pe.wait_ge(am["zT_ready"], 2 + t - 1)
                nc.tensor.transpose(small[t % 2][:, 0:P], h[:, t, :], ident).then_inc(am["zT_ps"], 1)
            pe.wait_ge(am["zT_ready"], 2 + T)
            for t in range(T):
                pe.wait_ge(s["uv_loaded"], 48)
                for w in range(2):
                    pe.wait_ge(am["G_taken"] if w else am["M_taken"], nth(t, 1))
                    for j in range(8):
                        last = nc.tensor.matmul(sc[w][:, P * j:P * j + P], uvT[:, w, P * j:P * j + P],
                                                hT[:, t, :], start=True, stop=True)
                    last.then_inc(am["uT_ps"], 1)
                for w in range(2):
                    pe.wait_ge(am["v2_taken"] if w else am["v12_taken"], nth(t, 1))
                    for i in range(2):
                        bank = pt[:, 512 * i:512 * i + 512] if w == 0 else small[i][:, :]
                        last = nc.tensor.matmul(bank, hT[:, t, :], uvT[:, w, 512 * i:512 * i + 512], start=True, stop=True)
                    last.then_inc(am["un_ps"], 1)
                pe.wait_ge(am["uT_half"], nth(t))
                pe.wait_ge(am["uT_taken"], nth(t))
                for w in range(2):
                    for p in range(2):
                        for j in range(8):
                            for b in range(2):
                                rows, tok = slice(R * p, R * p + R), slice(L * b, L * b + L)
                                last = nc.tensor.matmul(sc[w][L * b:L * b + L, 512 * p + L * j:512 * p + L * j + L],
                                                        ut[rows, w, j, tok], ut[rows, 1 - w, j, tok],
                                                        start=True, stop=True)
                        last.then_inc(am["M_ps"], 1)
                for w in range(2):
                    pe.wait_ge(am["un_half"], nth(t))
                    pe.wait_ge(am["un_taken"], nth(t))
                    pe.wait_ge(am["qh_ready"], nth(2 * t + 1))
                    for b in range(2):
                        for j in range(8):
                            for p in range(2):
                                c, rows = 2 * j + p, slice(L * b, L * b + L)
                                bank = pt[:, 512 * b:512 * b + 512] if w == 0 else small[b][:, :]
                                last = nc.tensor.matmul(bank[R * p:R * p + R, L * j:L * j + L],
                                                        un[rows, 1 - w, R * c:R * c + R], qh[rows, 1 - w, p, j, :],
                                                        start=True, stop=True)
                    last.then_inc(am["v12_ps"], 1)
                for w in range(2):
                    pe.wait_ge(am["v2_taken"] if w else am["v12_taken"], nth(t))
                    for j in range(8):
                        last = nc.tensor.matmul(sc[1][:, 0:P], v12[:, w, j, :, :].rearrange("p b q -> p (b q)"),
                                                uv[:, w, j, :], start=(w == 0 and j == 0), stop=(w == 1 and j == 7))
                last.then_inc(am["G_ps"], 1)
            pe.wait_ge(s["uv_loaded"], 48)
            for t in range(T):
                pe.wait_ge(s["ln_done"], 2 * T + t + 1)
                if t >= 2:
                    pe.wait_ge(am["zT_ready"], 2 + T + t - 1)
                nc.tensor.transpose(small[t % 2][:, 0:P], h[:, t, :], ident).then_inc(am["zT_ps"], 1)
            for t in range(T):
                pe.wait_ge(am["zT_ready"], 2 + T + t + 1)
                for i in range(2):
                    last = nc.tensor.matmul(pt[:, 512 * (t % 2):512 * (t % 2) + P] if t < 2 else sc[0][:, 512 * (t % 2):512 * (t % 2) + P],
                                            hT[:, t, :], ffw[:, i, :], start=(i == 0), stop=(i == 1))
                last.then_inc(am["F_ps"], 1)

        def am_act(act):
            for k in range(2):
                for t in range(T):
                    act.wait_ge(am["zT_ps"], 2 + k * T + t + 1)
                    if k == 0 or True:
                        nc.scalar.copy(hT[:, t, :], small[t % 2][:, 0:P]).then_inc(am["zT_ready"], 1)
                if k == 1:
                    break
                for t in range(T):
                    act.wait_ge(am["uT_ps"], nth(2 * t))
                    act.wait_ge(am["M_ps"], nth(4 * t, 1))
                    nc.scalar.mul(sd[:, 0, :], sc[0][:], UV_SCALE).then_inc(am["uT_half"], 1)
                    act.wait_ge(am["un_ps"], nth(2 * t))
                    act.wait_ge(am["v12_ps"], nth(2 * t, 1))
                    nc.scalar.mul(un[:, 0, :], pt[:], UV_SCALE).then_inc(am["un_half"], 1)
                    for w in range(2):
                        act.wait_ge(am["M_ps"], nth(4 * t + 2 * w + 1))
                        act.wait_ge(am["qh_ready"], nth(2 * t + w, 2))
                        nc.scalar.activation(th[:, w, :], sc[w][:], ACT.Tanh,
                                             scale=0.5).then_inc(am["M_taken"] if w == 0 else am["MT_taken"], 1)
                    act.wait_ge(am["v12_ps"], nth(2 * t + 1))
                    act.wait_ge(am["G_ps"], nth(t, 1))
                    for b in range(2):
                        last = nc.scalar.copy(v12[:, 1, :, b, :], small[b][:].rearrange("p (j q) -> p j q", q=L))
                    last.then_inc(am["v2_taken"], 1)

        def am_dve(dve):
            layernorm_dve(dve, 1, x, h)
            for t in range(T):
                dve.wait_ge(am["uT_ps"], nth(2 * t + 1))
                dve.wait_ge(am["M_ps"], nth(4 * t, 1))
                nc.vector.tensor_scalar(sd[:, 1, :], sc[1][:], UV_SCALE, None,
                                        ALU.mult).then_inc(am["uT_taken"], 1)
                dve.wait_ge(am["un_ps"], nth(2 * t + 1))
                dve.wait_ge(am["v12_ps"], nth(2 * t, 1))
                for i in range(2):
                    last = nc.vector.tensor_scalar(un[:, 1, 512 * i:512 * i + 512], small[i][:], UV_SCALE, None, ALU.mult)
                last.then_inc(am["un_taken"], 1)
                for w in range(2):
                    dve.wait_ge(am["M_taken"] if w == 0 else am["MT_taken"], nth(t))
                    nc.vector.tensor_scalar(pr[:, 2 + w, :], th[:, w, :], 0.5, 0.5, ALU.mult, ALU.add).then_inc(am["qh_ready"], 1)
                dve.wait_ge(am["v12_ps"], nth(2 * t))
                for b in range(2):
                    last = nc.vector.tensor_copy(v12[:, 0, :, b, :], pt[:, 512 * b:512 * b + 512].rearrange("p (j q) -> p j q", q=L))
                last.then_inc(am["v12_taken"], 1)
                dve.wait_ge(am["G_ps"], nth(t))
                xt = x[:, t, :]
                nc.vector.scalar_tensor_tensor(xt, sc[1][:, 0:P], UV_SCALE, xt, ALU.mult, ALU.add).then_inc(am["G_taken"], 1)
            dve.wait_ge(am["G_taken"], 2 + T)
            layernorm_dve(dve, 2, x, h)
            for t in range(T):
                dve.wait_ge(am["F_ps"], 2 + t + 1)
                bank = pt[:, 512 * (t % 2):512 * (t % 2) + P] if t < 2 else sc[0][:, 512 * (t % 2):512 * (t % 2) + P]
                nc.vector.tensor_tensor(x[:, t, :], bank, x[:, t, :], ALU.add).then_inc(am["F_taken"], 1)

        def am_pool(pool):
            layernorm_pool(pool, 1)
            layernorm_pool(pool, 2)

        with nc.Block() as block:
            block.tensor(am_pe)
            block.scalar(am_act)
            block.vector(am_dve)
            block.gpsimd(am_pool)
        if stop in (2, 3):
            return store_now()

        def renewed(stack, prefix, names, start=2):
            stack.close()
            new = {n: stack.enter_context(nc.semaphore(prefix + n)) for n in names}
            with nc.Block() as block:
                @block.gpsimd
                def _(pool):
                    for n in names:
                        pool.sem_clear(new[n])
                        pool.sem_inc(new[n], start)
            return new

        LEAD = 8

        def nth(k, back=0):
            return k + 1 + LEAD - back

        xm = renewed(early, "l1_", (

            "lnT_ps lnT_ready qkv_ps squared vl_ready sums floored rqk_ready q_scaled qT_ps q2T_ready gqk_ready qp_ps qp_act qp_dve slT_ps "
            "slT_ready sl_ps slat_ready bxb_ready bwv_ps bwv_ready mask_ready zeroed "
            "stats moments lg rstd centered xh_ready xT_ps xT_taken k_ps k_taken k_sum k_floored rk vl_copied sT_ps sT_taken s_ps max3 "
            "max1 max_neg exp PT_ps PT_act PT_dve U_ps U_taken rs_ctx rs_all rs4 O_ps rec o1 o2 o_done oT_ps oT_taken "
            "out_ps out_taken").split(), LEAD)


        def steps(eng, start, step, tail):
            start()
            with eng.Fori(0, (B - 2) // 2) as i:
                step(2 * i + 1, i, 1)
                step(2 * i + 2, i + 1, 0)
            step(B - 1, T - 1, 1)
            tail()

        def before(b, t, p):
            return b - 1, (t if p else t - 1), 1 - p

        def load_ctx(sp, b, p):
            lo = (CT - 1) * P
            src = ctx_in[ds(b, 1)]
            sp.dma_start(cx[p][:, 0:CT - 1, :], src[:, 0:lo, :].rearrange("a (p c) d -> p (a c) d", c=CT - 1)).then_inc(ctx_loaded[p], 16)
            sp.dma_start(cx[p][0:CR, CT - 1, :], src[:, lo:S2, :].rearrange("a p d -> p (a d)")).then_inc(ctx_loaded[p], 16)

        def x_sp(sp):
            sp.dma_start(xw[:], xw_in).then_inc(xw_loaded, 16)
            sp.dma_start(bout[:], bout_in.to_broadcast([P, D])).then_inc(xw_loaded, 16)
            sp.dma_start(eye2[:], eye2_in).then_inc(xw_loaded, 16)
            sp.dma_start(mraw[:], mask_in).then_inc(xw_loaded, 16)
            sp.dma_start(sel[:], sel_in).then_inc(xw_loaded, 16)
            sp.wait_ge(xm["zeroed"], LEAD + 4)
            load_ctx(sp, 0, 0)
            load_ctx(sp, 1, 1)
            with sp.Fori(0, (B - 2) // 2) as i:
                for p in range(2):
                    sp.wait_ge(xm["centered"], nth(4 * (2 * i + p) + 3))
                    load_ctx(sp, 2 * i + 2 + p, p)

        def x_pe_pre(pe):
            pe.wait_ge(xw_loaded, 80)
            for t in range(T):
                pe.wait_ge(s["ln_done"], 4 * T + t + 1)
                if t >= 2:
                    pe.wait_ge(xm["lnT_ready"], nth(t - 2))
                nc.tensor.transpose(small[t % 2][:, 0:P], o[:, t, :], ident).then_inc(xm["lnT_ps"], 1)
            for t in range(T):
                pe.wait_ge(xm["lnT_ready"], nth(t))
                for i, w in enumerate((X_Q, X_K, X_V)):
                    last = nc.tensor.matmul(sc[i // 2][:, 512 * (i % 2) + P * t:512 * (i % 2) + P * t + P], hT[:, t, :],
                                            xw[:, w:w + P], start=True, stop=True)
            last.then_inc(xm["qkv_ps"], 1)
            pe.wait_ge(xm["bxb_ready"], nth(0))
            nc.tensor.matmul(pt[:, 0:P], bxb[:], xw[:, X_V:X_V + P], start=True, stop=True).then_inc(xm["bwv_ps"], 1)
            pe.wait_ge(xm["q_scaled"], nth(0))
            for t in range(T):
                pe.wait_ge(xm["q2T_ready"], nth(t - 2)) if t >= 2 else None
                nc.tensor.transpose(small[t % 2][:, 0:P], qnat[:, t, :], ident).then_inc(xm["qT_ps"], 1)
            pe.wait_ge(xm["q2T_ready"], nth(T - 1))
            pe.wait_ge(xm["bwv_ready"], nth(0))
            for hh in range(XH):
                rows = slice(XD * hh, XD * hh + XD)
                last = nc.tensor.matmul(pt[:, 512 * hh:512 * hh + 512], xw[rows, X_KT:X_KT + P],
                                        qT[rows, :, :].rearrange("p t q -> p (t q)"), start=True, stop=True)
            last.then_inc(xm["qp_ps"], 1)
            pe.wait_ge(xm["qp_act"], nth(0))
            pe.wait_ge(xm["qp_dve"], nth(0))
            for b in range(B):
                t, p = b // 2, b % 2
                last = nc.tensor.matmul(sc[1][L * p:L * p + L, 512 + P * t:512 + P * t + P], hT[:, t, L * p:L * p + L],
                                        qp[:, b, :, :].rearrange("p h q -> p (h q)"), start=True, stop=True)
            last.then_inc(xm["slT_ps"], 1)
            pe.wait_ge(xm["slT_ready"], nth(0))
            for t in range(T):
                if t >= 2:
                    pe.wait_ge(xm["slat_ready"], nth(t - 2))
                nc.tensor.transpose(small[t % 2][:, 0:P], slt[:, t, :], ident).then_inc(xm["sl_ps"], 1)
            pe.wait_ge(xm["slat_ready"], nth(T - 1))
            pe.wait_ge(xm["vl_ready"], nth(0))

        def x_act_pre(act):
            act.wait_ge(xw_loaded, 80)
            for t in range(T):
                act.wait_ge(xm["lnT_ps"], nth(t))
                nc.scalar.activation(hT[:, t, :], small[t % 2][:, 0:P], ACT.Identity, scale=xw[:, X_GL:X_GL + 1],
                                     bias=xw[:, X_BL:X_BL + 1]).then_inc(xm["lnT_ready"], 1)
            act.wait_ge(xm["qkv_ps"], nth(0))
            nc.scalar.activation(sqx[:], sc[0][:], ACT.Square, scale=XD ** -0.5).then_inc(xm["squared"], 1)
            nc.scalar.copy(vl[:].rearrange("p t d -> p (t d)"), sc[1][:, 0:512]).then_inc(xm["vl_ready"], 1)
            act.wait_ge(xm["bwv_ps"], nth(0))
            nc.scalar.copy(bwv[:], pt[:, 0:P]).then_inc(xm["bwv_ready"], 1)
            act.wait_ge(xm["gqk_ready"], nth(0))
            for t in range(T):
                act.wait_ge(xm["qT_ps"], nth(t))
                nc.scalar.activation(qT[:, t, :], small[t % 2][:, 0:P], ACT.Copy, scale=gqk[:, 0:1]).then_inc(xm["q2T_ready"], 1)
            act.wait_ge(xm["qp_ps"], nth(0))
            nc.scalar.copy(qp[:, :, 0, :], pt[:, 0:512].rearrange("p (b q) -> p b q", q=L)).then_inc(xm["qp_act"], 1)
            for t in range(T):
                act.wait_ge(xm["sl_ps"], nth(t))
                nc.scalar.copy(slat[:, t, :], small[t % 2][:, 0:P]).then_inc(xm["slat_ready"], 1)

        def x_dve_pre(dve):
            layernorm_dve(dve, 3, x, h)
            dve.wait_ge(s["ln_done"], 4 * T)
            layernorm_dve(dve, 4, h, o)
            dve.wait_ge(xw_loaded, 80)
            nc.vector.tensor_copy(bxb[:], xw[:, X_BX:X_BX + 1].to_broadcast([P, P])).then_inc(xm["bxb_ready"], 1)
            nc.vector.scalar_tensor_tensor(gqk[:], xw[:, X_GQ:X_GQ + 1], XD ** -0.5, xw[:, X_GK:X_GK + 1], ALU.mult,
                                           ALU.mult).then_inc(xm["gqk_ready"], 1)
            nc.vector.tensor_scalar(notm[:], mraw[:], -1.0, 1.0, ALU.mult, ALU.add).then_inc(xm["mask_ready"], 1)
            nc.vector.tensor_tensor(x[:], x[:], bout[:].unsqueeze(1).to_broadcast([P, T, D]), ALU.add).then_inc(s["x_ready"], 1)
            dve.wait_ge(xm["squared"], nth(0))
            nc.vector.tensor_reduce(ssq[:], sqx[:].rearrange("p (a d) -> p a d", d=XD), AX, ALU.add).then_inc(xm["sums"], 1)
            dve.wait_ge(xm["sums"], nth(0))
            nc.vector.tensor_scalar(ssq[:], ssq[:], RMS_FLOOR, None, ALU.max).then_inc(xm["floored"], 1)
            dve.wait_ge(xm["rqk_ready"], nth(0))
            nc.vector.tensor_tensor(qnat[:].rearrange("p t (h d) -> p (t h) d", d=XD),
                                    sc[0][:, 0:512].rearrange("p (a d) -> p a d", d=XD),
                                    rqk[:, 0:8].unsqueeze(2).to_broadcast([P, 8, XD]), ALU.mult).then_inc(xm["q_scaled"], 1)
            dve.wait_ge(xm["qp_ps"], nth(0))
            nc.vector.tensor_copy(qp[:, :, 1, :], pt[:, 512:1024].rearrange("p (b q) -> p b q", q=L)).then_inc(xm["qp_dve"], 1)
            dve.wait_ge(xm["slT_ps"], nth(0))
            nc.vector.tensor_tensor(slt[:].rearrange("p t (h q) -> p (t h) q", q=L),
                                    sc[1][:, 512:1024].rearrange("p (a q) -> p a q", q=L),
                                    rqk[:, 8:16].unsqueeze(2).to_broadcast([P, 8, L]), ALU.mult).then_inc(xm["slT_ready"], 1)

        def x_pool_pre(pool):
            for i in range(2):
                nc.gpsimd.memset(cx[i][L:P, CT - 1, :], 0.0).then_inc(xm["zeroed"], 1)
            pool.wait_ge(xm["zeroed"], LEAD + 2)
            for i in range(2):
                nc.gpsimd.memset(pn[i][:, S2:(CT + 1) * P], 0.0).then_inc(xm["zeroed"], 1)
            layernorm_pool(pool, 3)
            layernorm_pool(pool, 4)
            pool.wait_ge(xm["floored"], nth(0))
            nc.gpsimd.tensor_tensor(rqk[:], ssq[:], par[:, 1:2].to_broadcast([P, 16]), ALU.pow).then_inc(xm["rqk_ready"], 1)

        def x_turn(pe, b, p, g):
            pe.wait_ge(xm["xh_ready"], nth(4 * b + g))
            pe.wait_ge(xm["xT_taken"], nth(4 * b + g, 1))
            if g == 0:
                pe.wait_ge(xm["o_done"], nth(b, 2))
                if p == 1:
                    pass
                pe.wait_ge(xm["out_taken"], nth_tile(b, p))
            for j, c in enumerate(CG[g]):
                last = nc.tensor.transpose(pt[:, P * j:P * j + P], xh[p][:, c, :], ident)
            last.then_inc(xm["xT_ps"], 1)

        def nth_tile(b, p):
            return XT[0] + LEAD

        def x_keys(pe, b, p, g):
            n = 4 * b + g
            pe.wait_ge(xm["xT_taken"], nth(n))
            pe.wait_ge(xm["k_taken"], nth(n, 1))
            pe.wait_ge(xm["sT_taken"], nth(n, 2))
            if g == 2:
                pe.wait_ge(xm["U_taken"], nth(b, 1))
            if g == 0:
                pe.wait_ge(xm["oT_taken"], XT[0] + LEAD)
            src = xnT[g % 2]
            for j, c in enumerate(CG[g]):
                last = nc.tensor.matmul(pt[:, 512 + P * j:512 + P * j + P], src[:, P * j:P * j + P], xw[:, X_K:X_K + P], start=True, stop=True)
            last.then_inc(xm["k_ps"], 1)
            pe.wait_ge(xm["mask_ready"], nth(0))
            for j, c in enumerate(CG[g]):
                bank = small[g % 2][:, P * j:P * j + P]
                nc.tensor.matmul(bank, notm[:, P * c:P * c + P], sel[:, ds(b, 1), :].rearrange("p a n -> p (a n)"), start=True, stop=True)
                last = nc.tensor.matmul(bank, src[:, P * j:P * j + P], qp[:, ds(b, 1), :, :].rearrange("p a h q -> p (a h q)"),
                                        start=False, stop=True, skip_group_check=True)
            last.then_inc(xm["sT_ps"], 1)

        def x_weights(pe, b, p, last_a):
            pe.wait_ge(xm["exp"], nth(b))
            for i in range(4):
                for c in range(4 * i, min(4 * i + 4, CT + 1)):
                    last = nc.tensor.transpose(sc[i // 2][:, P * (c % 8):P * (c % 8) + P], pn[p][:, P * c:P * c + P], ident)
                last.then_inc(xm["PT_ps"], 1)
            pe.wait_ge(xm["k_taken"], last_a)
            for c in range(CT):
                if c % 4 == 0:
                    i = c // 4
                    pe.wait_ge(xm["PT_act" if i < 2 else "PT_dve"], nth(2 * b + i % 2))
                last = nc.tensor.matmul(pt[:, 512:512 + P], xh[p][:, c, :], ptx[:, c, :], start=(c == 0), stop=(c == CT - 1))
            last.then_inc(xm["U_ps"], 1)

        def x_scores(pe, b):
            pe.wait_ge(xm["sT_taken"], nth(4 * b + 3))
            pe.wait_ge(xm["PT_act"], nth(2 * b + 1, 2))
            pe.wait_ge(xm["PT_dve"], nth(2 * b + 1, 2))
            for i in range(2):
                for c in range(8 * i, min(8 * i + 8, CT)):
                    last = nc.tensor.transpose(sc[i][:, P * (c % 8):P * (c % 8) + P], sT[:, c, :], ident)
                last.then_inc(xm["s_ps"], 1)

        def x_out(pe, b, t, p, last_a):
            pe.wait_ge(xm["U_taken"], nth(b))
            pe.wait_ge(xm["rs4"], nth(b))
            pe.wait_ge(xm["vl_copied"], nth(b))
            pe.wait_ge(xm["xT_taken"], last_a)
            rows = slice(L * p, L * p + L)
            for hh in range(XH):
                cols = slice(XD * hh, XD * hh + XD)
                nc.tensor.matmul(pt[rows, cols], utx[:, cols], xw[:, X_V + XD * hh:X_V + XD * hh + XD], start=True, stop=False)
                nc.tensor.matmul(pt[rows, cols], ptx[:, CT, cols], vlc[p][:, cols],
                                 start=False, stop=True)
            nc.tensor.matmul(pt[rows, P:P + 4], eye2[:], rs4[:].rearrange("p k h -> p (k h)"), start=True, stop=True).then_inc(xm["O_ps"], 1)
            if p == 1:
                pe.wait_ge(xm["o_done"], nth(b))
                nc.tensor.transpose(pt[:, 512:512 + P], ox[:], ident).then_inc(xm["oT_ps"], 1)
                pe.wait_ge(xm["oT_taken"], nth(t))
                nc.tensor.matmul(pt[:, 0:P], oTx[:], xw[:, X_O:X_O + P], start=True, stop=True).then_inc(xm["out_ps"], 1)

        XT = [0]

        def x_pe(pe):
            x_pe_pre(pe)

            def keys(b, p, mid):
                x_turn(pe, b, p, 0)
                x_turn(pe, b, p, 1)
                x_keys(pe, b, p, 0)
                x_turn(pe, b, p, 2)
                x_keys(pe, b, p, 1)
                mid()
                x_turn(pe, b, p, 3)
                x_keys(pe, b, p, 2)
                x_keys(pe, b, p, 3)

            def start():
                XT[0] = 0
                keys(0, 0, lambda: None)
                x_scores(pe, 0)

            def step(b, t, p):
                bb, tt, pp = before(b, t, p)
                XT[0] = t
                if p == 0:
                    XT[0] = t - 1
                keys(b, p, lambda: x_weights(pe, bb, pp, nth(4 * b + 1)))
                x_scores(pe, b)
                x_out(pe, bb, tt, pp, nth(4 * b + 3))

            def tail():
                x_weights(pe, B - 1, 1, nth(4 * B - 1))
                x_out(pe, B - 1, T - 1, 1, nth(4 * B - 1))

            steps(pe, start, step, tail)

        def x_turned(act, b, g):
            n, w = 4 * b + g, P * len(CG[g])
            act.wait_ge(xm["sT_ps"], nth(n, 2))
            act.wait_ge(xm["xT_ps"], nth(n))
            nc.scalar.activation(xnT[g % 2][:, 0:w], pt[:, 0:w], ACT.Identity, scale=xw[:, X_GX:X_GX + 1],
                                 bias=xw[:, X_BX:X_BX + 1]).then_inc(xm["xT_taken"], 1)

        def x_squares(act, b, g):
            n, w = 4 * b + g, P * len(CG[g])
            act.wait_ge(xm["k_sum"], nth(n, 2))
            act.wait_ge(xm["k_ps"], nth(n))
            nc.scalar.activation(ksq[g % 2][:, 0:w], pt[:, 512:512 + w], ACT.Square, scale=XD ** -0.5).then_inc(xm["k_taken"], 1)

        def x_exp(act, b, t, p):
            act.wait_ge(xm["PT_ps"], nth(4 * b + 3, 8))
            act.wait_ge(xm["rs4"], nth(b, 2))
            act.wait_ge(xm["max_neg"], nth(b))
            nc.scalar.activation(pn[p][:, 0:1024], sc[0][:], ACT.Exp, bias=nmx[p][:, 0:1], accum_out=rsum[p][:, 0:1])
            nc.scalar.activation(pn[p][:, 1024:S2], sc[1][:, 0:S2 - 1024], ACT.Exp, bias=nmx[p][:, 0:1], accum_out=rsum[p][:, 1:2])
            lat = CT * P + L * p
            nc.scalar.activation(pn[p][:, lat:lat + L], slat[:, ds(t, 1), L * p:L * p + L].rearrange("p a k -> p (a k)"), ACT.Exp,
                                 bias=nmx[p][:, 0:1], accum_out=rsum[p][:, 2:3]).then_inc(xm["exp"], 1)

        def x_weights_act(act, b):
            act.wait_ge(xm["O_ps"], nth(b, 1))
            for i in range(2):
                act.wait_ge(xm["PT_ps"], nth(4 * b + i))
                nc.scalar.copy(ptx[:, 4 * i:4 * i + 4, :].rearrange("p c q -> p (c q)"), sc[0][:, 512 * i:512 * i + 512]).then_inc(xm["PT_act"], 1)
            act.wait_ge(xm["U_ps"], nth(b))
            nc.scalar.activation(utx[:], pt[:, 512:512 + P], ACT.Copy, scale=xw[:, X_GX:X_GX + 1]).then_inc(xm["U_taken"], 1)

        def x_out_act(act, t, p):
            if p == 1:
                act.wait_ge(xm["out_ps"], nth(t, 1))
                act.wait_ge(xm["oT_ps"], nth(t))
                nc.scalar.copy(oTx[:], pt[:, 512:512 + P]).then_inc(xm["oT_taken"], 1)

        def x_act(act):
            x_act_pre(act)

            def keys(b, exp, mid):
                x_turned(act, b, 0)
                x_turned(act, b, 1)
                x_squares(act, b, 0)
                exp()
                x_turned(act, b, 2)
                x_squares(act, b, 1)
                mid()
                x_turned(act, b, 3)
                x_squares(act, b, 2)
                x_squares(act, b, 3)

            def start():
                keys(0, lambda: None, lambda: None)

            def step(b, t, p):
                bb, tt, pp = before(b, t, p)
                keys(b, lambda: x_exp(act, bb, tt, pp), lambda: x_weights_act(act, bb))
                x_out_act(act, tt, pp)

            def tail():
                x_exp(act, B - 1, T - 1, 1)
                x_weights_act(act, B - 1)
                x_out_act(act, T - 1, 1)

            steps(act, start, step, tail)

        def x_stats(dve, b, t, p):
            dve.wait_ge(xm["xh_ready"], nth(4 * b + 3, 8))
            dve.wait_ge(ctx_loaded[p], 32 * t + 32)
            for c in range(CT):
                last = nc.vector.bn_stats(stx[:, c, :], cx[p][:, c, :])
            last.then_inc(xm["stats"], 1)
            dve.wait_ge(xm["stats"], nth(b))

        def x_moments(dve, b, p):
            for c in range(CT):
                last = nc.vector.bn_aggr(mvx[p][:, c, :], stx[:, c, :])
            last.then_inc(xm["moments"], 1)

        def x_sums(dve, b, g):
            n, k, i = 4 * b + g, 2 * len(CG[g]), g % 2
            dve.wait_ge(xm["k_taken"], nth(n))
            nc.vector.tensor_reduce(kss[i][:, 0:k], ksq[i][:, 0:XD * k].rearrange("p (a d) -> p a d", d=XD), AX, ALU.add).then_inc(xm["k_sum"], 1)
            dve.wait_ge(xm["k_sum"], nth(n))
            nc.vector.tensor_scalar(kfl[i][:, 0:k], kss[i][:, 0:k], RMS_FLOOR, None, ALU.max).then_inc(xm["k_floored"], 1)

        def x_scaled(dve, b, g):
            n, k, i = 4 * b + g, 2 * len(CG[g]), g % 2
            dve.wait_ge(xm["rk"], nth(n))
            dve.wait_ge(xm["sT_ps"], nth(n))
            nc.vector.tensor_tensor(sT[:, CG[g][0]:CG[g][-1] + 1, :].rearrange("p c (h q) -> p (c h) q", q=L),
                                    small[i][:, 0:L * k].rearrange("p (a q) -> p a q", q=L),
                                    rk[i][:, 0:k].unsqueeze(2).to_broadcast([P, k, L]), ALU.mult).then_inc(xm["sT_taken"], 1)

        def x_max(dve, b, t, p):
            nc.vector.tensor_reduce(mxx[:, 2:3], slat[:, ds(t, 1), L * p:L * p + L].rearrange("p a k -> p (a k)"), AX, ALU.max)
            dve.wait_ge(xm["s_ps"], nth(2 * b))
            nc.vector.tensor_reduce(mxx[:, 0:1], sc[0][:], AX, ALU.max)
            dve.wait_ge(xm["s_ps"], nth(2 * b + 1))
            nc.vector.tensor_reduce(mxx[:, 1:2], sc[1][:, 0:S2 - 1024], AX, ALU.max).then_inc(xm["max3"], 1)
            dve.wait_ge(xm["max3"], nth(b))
            nc.vector.tensor_reduce(mx1[:], mxx[:], AX, ALU.max).then_inc(xm["max1"], 1)
            dve.wait_ge(xm["max1"], nth(b))
            nc.vector.tensor_scalar(nmx[p][:], mx1[:], -1.0, None, ALU.mult).then_inc(xm["max_neg"], 1)

        def x_weights_dve(dve, b, p):
            dve.wait_ge(xm["O_ps"], nth(b, 1))
            dve.wait_ge(xm["exp"], nth(b))
            nc.vector.tensor_tensor(rc[:, 0:1], rsum[p][:, 0:1], rsum[p][:, 1:2], ALU.add).then_inc(xm["rs_ctx"], 1)
            dve.wait_ge(xm["rs_ctx"], nth(b))
            nc.vector.tensor_tensor(rc[:, 1:2], rc[:, 0:1], rsum[p][:, 2:3], ALU.add).then_inc(xm["rs_all"], 1)
            dve.wait_ge(xm["rs_all"], nth(b))
            nc.vector.tensor_tensor(rs4[:], rc[:].unsqueeze(2).to_broadcast([P, 2, 2]), vm2.unsqueeze(1).to_broadcast([P, 2, 2]),
                                    ALU.mult).then_inc(xm["rs4"], 1)
            for i in range(2):
                n = min(4, CT + 1 - (8 + 4 * i))
                dve.wait_ge(xm["PT_ps"], nth(4 * b + 2 + i))
                nc.vector.tensor_copy(ptx[:, 8 + 4 * i:8 + 4 * i + n, :].rearrange("p c q -> p (c q)"),
                                      sc[1][:, 512 * i:512 * i + P * n]).then_inc(xm["PT_dve"], 1)

        def x_out_dve(dve, b, t, p):
            rows = slice(L * p, L * p + L)
            heads = "p (h d) -> p h d"
            dve.wait_ge(xm["O_ps"], nth(b))
            nc.vector.reciprocal(rec[rows, :], pt[rows, P + 2:P + 4]).then_inc(xm["rec"], 1)
            nc.vector.tensor_tensor(o1[rows, :].rearrange(heads, d=XD), bwv[rows, :].rearrange(heads, d=XD),
                                    pt[rows, P:P + 2].unsqueeze(2).to_broadcast([L, 2, XD]), ALU.mult).then_inc(xm["o1"], 1)
            dve.wait_ge(xm["o1"], nth(b))
            nc.vector.tensor_tensor(o2[rows, :], o1[rows, :], pt[rows, 0:P], ALU.add).then_inc(xm["o2"], 1)
            dve.wait_ge(xm["rec"], nth(b))
            dve.wait_ge(xm["o2"], nth(b))
            nc.vector.tensor_tensor(ox[rows, :].rearrange(heads, d=XD), o2[rows, :].rearrange(heads, d=XD),
                                    rec[rows, :].unsqueeze(2).to_broadcast([L, 2, XD]), ALU.mult).then_inc(xm["o_done"], 1)
            if p == 1:
                dve.wait_ge(xm["out_ps"], nth(t))
                xt = x[:, ds(t, 1), :].rearrange("p a q -> p (a q)")
                nc.vector.tensor_tensor(xt, pt[:, 0:P], xt, ALU.add).then_inc(xm["out_taken"], 1)

        def x_dve(dve):
            x_dve_pre(dve)
            x_stats(dve, 0, 0, 0)
            x_moments(dve, 0, 0)

            def keys(b, t, p, mid, more=True):
                x_sums(dve, b, 0)
                x_sums(dve, b, 1)
                x_scaled(dve, b, 0)
                mid()
                x_scaled(dve, b, 1)
                if more:
                    x_stats(dve, b + 1, t + p, 1 - p)
                x_sums(dve, b, 2)
                if more:
                    x_moments(dve, b + 1, 1 - p)
                x_sums(dve, b, 3)
                x_scaled(dve, b, 2)
                x_scaled(dve, b, 3)
                x_max(dve, b, t, p)

            def start():
                dve.wait_ge(xm["slat_ready"], nth(T - 1))
                dve.wait_ge(xm["bwv_ready"], nth(0))
                keys(0, 0, 0, lambda: None)

            def step(b, t, p):
                bb, tt, pp = before(b, t, p)
                keys(b, t, p, lambda: x_weights_dve(dve, bb, pp), more=not (isinstance(b, int) and b == B - 1))
                x_out_dve(dve, bb, tt, pp)

            def tail():
                x_weights_dve(dve, B - 1, 1)
                x_out_dve(dve, B - 1, T - 1, 1)

            steps(dve, start, step, tail)

        def x_rstd(pool, b, p):
            pool.wait_ge(xm["moments"], nth(b))
            nc.gpsimd.tensor_tensor(lgx[:], mvx[p][:, :, 1], par[:, 0:1].to_broadcast([P, CT]), ALU.add).then_inc(xm["lg"], 1)
            pool.wait_ge(xm["lg"], nth(b))
            nc.gpsimd.tensor_tensor(rsx[p][:], lgx[:], par[:, 1:2].to_broadcast([P, CT]), ALU.pow).then_inc(xm["rstd"], 1)

        def x_normed(pool, b, p, g):
            c = CG[g]
            tiles, shape = slice(c[0], c[-1] + 1), [P, len(c), D]
            if g == 0:
                pool.wait_ge(xm["U_ps"], nth(b, 2))
            nc.gpsimd.tensor_tensor(xh[p][:, tiles, :], cx[p][:, tiles, :], mvx[p][:, tiles, 0].unsqueeze(2).to_broadcast(shape),
                                    ALU.subtract).then_inc(xm["centered"], 1)
            pool.wait_ge(xm["rstd"], nth(b))
            pool.wait_ge(xm["centered"], nth(4 * b + g))
            nc.gpsimd.tensor_tensor(xh[p][:, tiles, :], xh[p][:, tiles, :], rsx[p][:, tiles].unsqueeze(2).to_broadcast(shape),
                                    ALU.mult).then_inc(xm["xh_ready"], 1)

        def x_rk(pool, b, g):
            n, k, i = 4 * b + g, 2 * len(CG[g]), g % 2
            pool.wait_ge(xm["k_floored"], nth(n))
            nc.gpsimd.tensor_tensor(rk[i][:, 0:k], kfl[i][:, 0:k], par[:, 1:2].to_broadcast([P, k]), ALU.pow).then_inc(xm["rk"], 1)

        def x_pool(pool):
            x_pool_pre(pool)
            pool.wait_ge(xm["vl_ready"], nth(0))
            x_rstd(pool, 0, 0)
            for g in range(4):
                x_normed(pool, 0, 0, g)

            def step(b, t, p):
                more = not (isinstance(b, int) and b == B - 1)
                x_rk(pool, b, 0)
                x_rk(pool, b, 1)
                pool.wait_ge(xm["O_ps"], nth(b, 2))
                nc.gpsimd.tensor_tensor(vlc[p][:], vl[:, ds(t, 1), :].rearrange("p a d -> p (a d)"),
                                        par[:, 2:3].to_broadcast([P, P]), ALU.mult).then_inc(xm["vl_copied"], 1)
                if more:
                    x_rstd(pool, b + 1, 1 - p)
                    x_normed(pool, b + 1, 1 - p, 0)
                x_rk(pool, b, 2)
                x_rk(pool, b, 3)
                if more:
                    for g in range(1, 4):
                        x_normed(pool, b + 1, 1 - p, g)

            steps(pool, lambda: step(0, 0, 0), step, lambda: None)

        with nc.Block() as block:
            block.sync(x_sp)
            block.tensor(x_pe)
            block.scalar(x_act)
            block.vector(x_dve)
            block.gpsimd(x_pool)
        if stop == 4:
            return store_now()

        ms = renewed(early, "moe_", (
            "hT_ps hT_ready logits_ps logits gate_max gate_shifted gate_exp gate_sum gate_rec probs best rank first picked dropped chosen choT_ps "
            "choT_ready b2_ps x_b2 up_ps relu_act relu_dve down_ps x_added").split(), LEAD)

        def load_expert(sp, e, p):
            sp.dma_start(we[p][:], we_in[ds(e, 1)].rearrange("a p n -> p (a n)")).then_inc(expert_loaded[p], 16)

        with nc.Block() as block:
            @block.sync
            def _(sp):
                sp.dma_start(gate[:], gate_in).then_inc(gate_loaded, 16)
                sp.dma_start(b2[:], b2_in).then_inc(gate_loaded, 16)
                load_expert(sp, 0, 0)
                load_expert(sp, 1, 1)

            @block.tensor
            def _(pe):
                layer(pe_stage, pe, LAST, LAYERS)

            @block.scalar
            def _(act):
                layer(act_stage, act, LAST, LAYERS)

            @block.vector
            def _(dve):
                layernorm_dve(dve, 5, x, h, s["h_ready"])
                layer(dve_stage, dve, LAST, LAYERS)

            @block.gpsimd
            def _(pool):
                layernorm_pool(pool, 5)
                layer(pool_stage, pool, LAST, LAYERS)
        if stop == 5:
            return store_now()

        def e_up(pe, e, t, p):
            pe.wait_ge(expert_loaded[p], 16 * t + 16)
            for c in range(FC):
                pe.wait_ge(ms["relu_act" if c < 2 else "relu_dve"], nth(2 * e + c % 2, 2))
                nc.tensor.matmul(sc[c // 2][:, 512 * (c % 2):512 * (c % 2) + 512], we[p][:, W_1 + P * c:W_1 + P * c + P],
                                 hT[:].rearrange("p t q -> p (t q)"), start=True, stop=True).then_inc(ms["up_ps"], 1)

        def e_down(pe, e, p):
            pe.wait_ge(ms["relu_act"], nth(2 * e + 1))
            pe.wait_ge(ms["relu_dve"], nth(2 * e + 1))
            pe.wait_ge(ms["x_added"], nth(T * e + T - 1, 2 * T))
            for t in range(T):
                for c in range(FC):
                    last = nc.tensor.matmul(pt[:, 512 * p + P * t:512 * p + P * t + P], hid[p][:, c, P * t:P * t + P],
                                            we[p][:, W_2 + P * c:W_2 + P * c + P], start=(c == 0), stop=(c == FC - 1))
            last.then_inc(ms["down_ps"], 1)

        def experts(eng, up, down):
            up(0, 0, 0)
            with eng.Fori(0, E // 2 - 1) as i:
                up(2 * i + 1, i, 1)
                down(2 * i, 0)
                up(2 * i + 2, i + 1, 0)
                down(2 * i + 1, 1)
            up(E - 1, E // 2 - 1, 1)
            down(E - 2, 0)
            down(E - 1, 1)

        def e_sp(sp):
            with sp.Fori(0, E // 2 - 1) as i:
                for p in range(2):
                    sp.wait_ge(ms["down_ps"], nth(2 * i + p))
                    load_expert(sp, 2 * i + 2 + p, p)

        def e_pe(pe):
            for t in range(T):
                pe.wait_ge(s["ln_done"], 5 * T + t + 1)
                if t >= 2:
                    pe.wait_ge(ms["hT_ready"], nth(t - 2))
                nc.tensor.transpose(small[t % 2][:, 0:P], h[:, t, :], ident).then_inc(ms["hT_ps"], 1)
            pe.wait_ge(ms["hT_ready"], nth(T - 1))
            pe.wait_ge(gate_loaded, 32)
            for t in range(T):
                last = nc.tensor.matmul(small[0][:, E * t:E * t + E], hT[:, t, :], gate[:, 0:E], start=True, stop=True)
            last.then_inc(ms["logits_ps"], 1)
            e_up(pe, 0, 0, 0)
            pe.wait_ge(ms["chosen"], nth(0))
            for t in range(T):
                last = nc.tensor.transpose(small[1][0:E, P * t:P * t + P], chosen[:, t, :], ident)
            last.then_inc(ms["choT_ps"], 1)
            pe.wait_ge(ms["choT_ready"], nth(0))
            for t in range(T):
                last = nc.tensor.matmul(small[1][:, P * t:P * t + P], choT[:, t, :], b2[:], start=True, stop=True)
            last.then_inc(ms["b2_ps"], 1)
            experts(pe, lambda e, t, p: None if isinstance(e, int) and e == 0 else e_up(pe, e, t, p), lambda e, p: e_down(pe, e, p))

        def e_act(act):
            for t in range(T):
                act.wait_ge(ms["hT_ps"], nth(t))
                nc.scalar.copy(hT[:, t, :], small[t % 2][:, 0:P]).then_inc(ms["hT_ready"], 1)
            act.wait_ge(ms["gate_shifted"], nth(0))
            nc.scalar.activation(gex[:], gsh[:], ACT.Exp).then_inc(ms["gate_exp"], 1)

            def relu(e, t, p):
                if isinstance(e, int) and e == 0:
                    act.wait_ge(ms["choT_ps"], nth(0))
                    nc.scalar.copy(choT[:].rearrange("p t q -> p (t q)"), small[1][0:E, :]).then_inc(ms["choT_ready"], 1)
                act.wait_ge(ms["down_ps"], nth(e, 2))
                for c in range(2):
                    act.wait_ge(ms["up_ps"], nth(4 * e + c))
                    nc.scalar.activation(hid[p][:, c, :], sc[0][:, 512 * c:512 * c + 512], ACT.Relu,
                                         bias=we[p][:, W_B1 + c:W_B1 + c + 1]).then_inc(ms["relu_act"], 1)

            experts(act, relu, lambda e, p: None)

        def e_choice(dve):
            each = [P, T, E]
            dve.wait_ge(gate_loaded, 32)
            dve.wait_ge(ms["logits_ps"], nth(0))
            nc.vector.tensor_tensor(lgt[:], small[0][:, 0:T * E].rearrange("p (t e) -> p t e", e=E),
                                    gate[:, E:2 * E].unsqueeze(1).to_broadcast(each), ALU.add).then_inc(ms["logits"], 1)
            dve.wait_ge(ms["logits"], nth(0))
            nc.vector.tensor_reduce(gmx[:], lgt[:], AX, ALU.max).then_inc(ms["gate_max"], 1)
            dve.wait_ge(ms["gate_max"], nth(0))
            nc.vector.tensor_tensor(gsh[:], lgt[:], gmx[:].unsqueeze(2).to_broadcast(each), ALU.subtract).then_inc(ms["gate_shifted"], 1)
            dve.wait_ge(ms["gate_exp"], nth(0))
            nc.vector.tensor_reduce(gsum[:], gex[:], AX, ALU.add).then_inc(ms["gate_sum"], 1)
            dve.wait_ge(ms["gate_sum"], nth(0))
            nc.vector.reciprocal(grec[:], gsum[:]).then_inc(ms["gate_rec"], 1)
            dve.wait_ge(ms["gate_rec"], nth(0))
            nc.vector.tensor_tensor(prob[0][:], gex[:], grec[:].unsqueeze(2).to_broadcast(each), ALU.mult).then_inc(ms["probs"], 1)
            dve.wait_ge(ms["probs"], nth(0))
            for k in range(2):
                nc.vector.tensor_reduce(best[:], prob[k][:], AX, ALU.max).then_inc(ms["best"], 1)
                dve.wait_ge(ms["best"], nth(3 * k))
                nc.vector.tensor_tensor(rank[:], prob[k][:], best[:].unsqueeze(2).to_broadcast(each), ALU.is_equal).then_inc(ms["best"], 1)
                dve.wait_ge(ms["best"], nth(3 * k + 1))
                nc.vector.tensor_tensor(rank[:], rank[:], gate[:, 2 * E:3 * E].unsqueeze(1).to_broadcast(each), ALU.mult).then_inc(ms["best"], 1)
                dve.wait_ge(ms["best"], nth(3 * k + 2))
                nc.vector.tensor_reduce(first[:], rank[:], AX, ALU.max).then_inc(ms["first"], 1)
                dve.wait_ge(ms["first"], nth(k))
                nc.vector.tensor_tensor(picked[k][:], rank[:], first[:].unsqueeze(2).to_broadcast(each), ALU.is_equal).then_inc(ms["picked"], 1)
                dve.wait_ge(ms["picked"], nth(k))
                if k == 0:
                    nc.vector.scalar_tensor_tensor(prob[1][:], picked[0][:], -2.0, prob[0][:], ALU.mult, ALU.add).then_inc(ms["dropped"], 1)
                    dve.wait_ge(ms["dropped"], nth(0))
            nc.vector.tensor_tensor(chosen[:], picked[0][:], picked[1][:], ALU.add).then_inc(ms["chosen"], 1)

        def e_dve(dve):
            layernorm_dve(dve, 6, x, h)
            e_choice(dve)

            def relu(e, t, p):
                dve.wait_ge(ms["down_ps"], nth(e, 2))
                for c in range(2, FC):
                    dve.wait_ge(ms["up_ps"], nth(4 * e + c))
                    nc.vector.tensor_scalar(hid[p][:, c, :], sc[1][:, 512 * (c - 2):512 * (c - 2) + 512],
                                            we[p][:, W_B1 + c:W_B1 + c + 1], 0.0, ALU.add, ALU.max).then_inc(ms["relu_dve"], 1)
                if isinstance(e, int) and e == 0:
                    dve.wait_ge(ms["b2_ps"], nth(0))
                    nc.vector.tensor_tensor(x[:].rearrange("p t d -> p (t d)"), small[1][:], x[:].rearrange("p t d -> p (t d)"),
                                            ALU.add).then_inc(ms["x_b2"], 1)
                    dve.wait_ge(ms["x_b2"], nth(0))

            def add(e, p):
                dve.wait_ge(ms["x_added"], nth(T * e, 1))
                dve.wait_ge(ms["down_ps"], nth(e))
                for t in range(T):
                    nc.vector.scalar_tensor_tensor(x[:, t, :], pt[:, 512 * p + P * t:512 * p + P * t + P],
                                                   chosen[:, t, ds(e, 1)], x[:, t, :], ALU.mult, ALU.add).then_inc(ms["x_added"], 1)

            experts(dve, relu, add)

        with nc.Block() as block:
            block.sync(e_sp)
            block.tensor(e_pe)
            block.scalar(e_act)
            block.vector(e_dve)

            @block.gpsimd
            def _(pool):
                layernorm_pool(pool, 6)

        store_now()


def constants():
    p = np.arange(P)
    cf = np.zeros((P, 155), np.float32)
    cf[:, :128] = np.eye(P)
    cf[:, 128:132] = (p[:, None] // HD) % 4 == np.arange(4)
    cf[:, 132:134] = p[:, None] // L == np.arange(2)
    cf[:, 134:138] = p[:, None] // KF == np.arange(4)
    cf[:, 138:154] = p[:, None] // HD == np.arange(16)
    cf[:, 154] = p
    j = np.arange(L)
    cb = np.zeros((L, P + 1024), np.float32)
    cb[:, :P] = np.where(j[:, None] > np.arange(P) % L, NEG, 0.0)
    cb[:, P:P + 512] = j[:, None] == np.arange(512) % L
    cb[:KF, P + 512:] = np.arange(KF)[:, None] == np.arange(512) % KF
    inv = (1.0 / np.float32(10000.0) ** (np.arange(0, HD, 2, dtype=np.float32) / np.float32(HD))).astype(np.float32)
    f = np.arange(L, dtype=np.float32)[:, None] * inv[None, :]
    emb = np.concatenate([f, f], axis=-1)
    cos, sin = np.cos(emb).T.astype(np.float32), np.sin(emb).T.astype(np.float32)
    sin = sin * np.where(np.arange(HD) < HD // 2, -1, 1)[:, None].astype(np.float32)
    cos, sin = np.tile(cos, (H, 2)), np.tile(sin, (H, 2))
    scale = np.float32(HD ** -0.5)
    trig = np.stack([cos * scale, sin * scale, cos, sin], axis=1).astype(np.float32)
    iota = np.arange(S2, dtype=np.float32)[None, :]
    eye2 = np.tile(np.eye(L, dtype=np.float32), (2, 1))
    sel = np.zeros((B, B, P), np.float32)
    sel[np.arange(B), np.arange(B)] = NEG
    return cf, cb.astype(mybir.dt.np(BF16)), trig, iota, eye2, sel.astype(mybir.dt.np(BF16))


def layout(i):
    i = {k: np.asarray(v) for k, v in i.items()}
    turn = (np.arange(P) // HD) * HD + (np.arange(P) % HD + HD // 2) % HD
    cf, cb, trig, iota, eye2, sel = constants()
    one_, zero = np.ones((1, P), np.float32), np.zeros((1, P), np.float32)
    wqkv = np.concatenate([i["L0_xattn_Wqkv"], i["L1_attn_w_qkv"][None]])
    wo = np.concatenate([i["L0_xattn_Wo"], i["L1_attn_w_out"][None]])
    n1 = np.concatenate([i["L0_xattn_n1"], one_])
    bq = np.concatenate([i["L0_xattn_bqkv"], np.zeros((1, 3 * P), np.float32)])
    bo = np.concatenate([i["L0_xattn_bo"], zero])
    q, k, v = wqkv[:, :P], wqkv[:, P:2 * P], wqkv[:, 2 * P:]
    wt = lambda a: a.transpose(0, 2, 1)
    col = lambda a: a[:, :, None]
    wa = np.concatenate([wt(q), wt(q[:, turn]), wt(k), wt(k[:, turn]), wt(v), wt(wo), col(n1), col(bq[:, :P]),
                         col(bq[:, :P][:, turn]), col(bq[:, P:2 * P]), col(bq[:, P:2 * P][:, turn]), col(bq[:, 2 * P:])], 2)
    wkv = i["L0_xattn_Wkv_c"]
    wb = np.concatenate([wt(i["L0_xattn_Wq_c"]), wt(wkv[:, :P]), wt(wkv[:, P:]), wt(i["L0_xattn_Wo_c"]),
                         col(i["L0_xattn_n2"])], 2)
    wd = wt(i["L0_xattn_Wd"]).reshape(LAYERS, FC, P, P).transpose(0, 2, 1, 3).reshape(LAYERS, P, F)
    wc = np.concatenate([wt(i["L0_xattn_Wg"]), wt(i["L0_xattn_Wu"]), wd, col(i["L0_xattn_n3"])], 2)
    c = i["ctx_1024"]
    u, v = i["L0_attn_ternary_factor_u"], i["L0_attn_ternary_factor_v"]
    uvT = np.stack([u.T, v.T], 1)
    uv = np.stack([u.reshape(8, P, D), v.reshape(8, P, D)]).transpose(2, 0, 1, 3)
    ffw = np.stack([i["L0_ffn_weight"].T, np.concatenate([i["L0_ffn_disha"]] * 2)], 1)
    wkv1 = i["L1_xattn_W_kv"]
    xcols = [i["L1_xattn_ln_x_g"], i["L1_xattn_ln_x_b"], i["L1_xattn_ln_l_g"], i["L1_xattn_ln_l_b"],
             np.tile(i["L1_xattn_q_gamma"], XH), np.tile(i["L1_xattn_k_gamma"], XH)]
    xw = np.concatenate([i["L1_xattn_W_q"], wkv1[:, :P], wkv1[:, P:], wkv1[:, :P].T, i["L1_xattn_W_out"], np.stack(xcols, 1)], 1)
    lo = (CT - 1) * P
    key = np.concatenate([(np.arange(P)[None] * (CT - 1) + np.arange(CT - 1)[:, None]).reshape(-1), np.arange(lo, S2)])
    mask = np.zeros((B, CT * P), bool)
    mask[:, :S2] = i["mask_BxS2_bk0"][:, key]
    bc = lambda a: np.broadcast_to(a, (P, E))
    gate = np.concatenate([i["L1_ffn_gate_w"], bc(i["L1_ffn_gate_b"]), bc((E - np.arange(E)).astype(np.float32))], 1)
    chunks = lambda a: a.reshape(E, FC, P, -1).transpose(0, 2, 1, 3).reshape(E, P, -1)
    we = np.concatenate([i["L1_ffn_w1"], chunks(i["L1_ffn_w2"]), chunks(i["L1_ffn_b1"])], 2)
    return dict(
        gate_in=gate, b2_in=i["L1_ffn_b2"], we_in=we,
        xw_in=xw, bout_in=i["L1_xattn_b_out"][None], eye2_in=eye2, mask_in=mask, sel_in=sel,
        x_in=i["x"].reshape(B * L, D), seg_in=i["itok_BxS_0_255"].reshape(1, B * L),
        segq_in=i["itok_BxS_0_255"].T, ctx_in=c, ctxT_in=c.transpose(0, 2, 1),
        memT_in=c[:, :KF].transpose(2, 0, 1), wa_in=wa, bo_in=bo, wb_in=wb, wc_in=wc, nf_in=i["L0_xattn_nf"][None],
        trig_in=trig, cf_in=cf, cb_in=cb, iota_in=iota, uvT_in=uvT, uv_in=uv, ffw_in=ffw)


def kernel(**inputs):
    from concourse import bacc, mybir as types
    from concourse.bass_utils import run_bass_kernel_spmd as launch

    nc = bacc.Bacc("TRN2", target_bir_lowering=False, num_devices=1)
    arrays = {name: np.ascontiguousarray(a) for name, a in layout(inputs).items()}
    args = {name: nc.dram_tensor(name, a.shape, types.dt.from_np(a.dtype), kind="ExternalInput").ap()
            for name, a in arrays.items()}
    args["out"] = nc.dram_tensor("out", (B * L, D), F32, kind="ExternalOutput").ap()
    program(nc, **args)
    result = launch(nc, [arrays], core_ids=[0])
    return result.results[0]["out"].reshape(B, L, D)
```
